# Optimizing a Trainium2 kernel written in Bass

```python
import numpy as np
import jax
import jax.numpy as jnp

def _softmax(x, axis=-1):
    return jax.nn.softmax(x, axis=axis)

def _gelu(x):
    return jax.nn.gelu(x, approximate=True)

def _silu(x):
    return jax.nn.silu(x)

def _sigmoid(x):
    return jax.nn.sigmoid(x)

def _layernorm(x, axis=-1, eps=1e-05):
    m = jnp.mean(x, axis=axis, keepdims=True)
    v = jnp.var(x, axis=axis, keepdims=True)
    return (x - m) / jnp.sqrt(v + eps)

def _scatter_add(tgt, idx, src, axis=0):
    return tgt.at[idx].add(src)

def _segment_sum(src, seg, n):
    return jax.ops.segment_sum(src, seg, n)
kernel_name = 'mk_seq_preln_d2_jaxref_r8_06795c'

def setup_inputs(seed: int=0):
    np.random.seed(seed)
    _w = jnp.asarray

    def _L0_attn_setup():
        import jax, jax.numpy as jnp
        import numpy as np
        B, S, E, H, D = (1, 256, 128, 16, 64)
        LAM_INIT = 0.8
        LN_EPS = 1e-05
        key = jax.random.key(seed)
        ks = jax.random.split(key, 6)
        w = 0.02
        return {'X': jax.random.normal(ks[0], (B, S, E), dtype=jnp.float32), 'Wq': jax.random.normal(ks[1], (H, E, 2 * D), dtype=jnp.float32) * w, 'bq': jnp.zeros((H, 2 * D), dtype=jnp.float32), 'Wk': jax.random.normal(ks[2], (H, E, 2 * D), dtype=jnp.float32) * w, 'bk': jnp.zeros((H, 2 * D), dtype=jnp.float32), 'Wv': jax.random.normal(ks[3], (H, E, D), dtype=jnp.float32) * w, 'bv': jnp.zeros((H, D), dtype=jnp.float32), 'Wo': jax.random.normal(ks[4], (H * D, E), dtype=jnp.float32) * w, 'bo': jnp.zeros((E,), dtype=jnp.float32), 'gamma': jnp.ones((E,), dtype=jnp.float32), 'beta': jnp.zeros((E,), dtype=jnp.float32), 'lam': jnp.float32(0.5)}
    _L0_attn_in = _L0_attn_setup()

    def _L0_ffn_setup():
        import jax, jax.numpy as jnp
        import numpy as np
        EPS = 1e-05

        def _ln(x, g, b):
            mu = jnp.mean(x, axis=-1, keepdims=True)
            var = jnp.mean(jnp.square(x - mu), axis=-1, keepdims=True)
            return (x - mu) * jax.lax.rsqrt(var + EPS) * g + b

        def _forward(x, index_b, index_t, sw1, sb1, sw2, sb2, sw3, sb3, s_ln_g, s_ln_b, sg_w, sg_b, eg_w, eg_b, exp_bias, ew1, eb1, ew2, eb2, ew3, eb3, sel_ln_g, sel_ln_b):
            x1 = jnp.einsum('btd,hd->bth', x, sw1) + sb1
            x2 = jnp.einsum('btd,hd->bth', x, sw2) + sb2
            sh = _ln(jax.nn.silu(x1) * x2, s_ln_g, s_ln_b)
            shared_out = jnp.einsum('bth,dh->btd', sh, sw3) + sb3
            x_moe = x[index_b, index_t]
            shared_scores = jax.nn.sigmoid(x_moe @ sg_w.T + sg_b)
            expert_scores = jax.nn.sigmoid(x_moe @ eg_w.T + eg_b)
            top1_idx = jnp.argmax(expert_scores + exp_bias, axis=-1)
            top1_score = jnp.take_along_axis(expert_scores, top1_idx[:, None], axis=-1)
            weights = jax.nn.softmax(jnp.concatenate([shared_scores, top1_score], axis=-1), axis=-1)
            shared_w, expert_w = (weights[:, 0], weights[:, 1])
            shared_moe_out = shared_out[index_b, index_t] * shared_w[:, None]
            h1 = jnp.einsum('md,ehd->meh', x_moe, ew1) + eb1
            h2 = jnp.einsum('md,ehd->meh', x_moe, ew2) + eb2
            z = _ln(jax.nn.silu(h1) * h2, sel_ln_g, sel_ln_b)
            out_all = jnp.einsum('meh,edh->med', z, ew3) + eb3
            expert_out = jnp.take_along_axis(out_all, top1_idx[:, None, None], axis=1)[:, 0]
            expert_moe_out = expert_out * expert_w[:, None]
            final_out = shared_out.at[index_b, index_t].set(shared_moe_out + expert_moe_out)
            return final_out
        B, T, D, E, H, M = (2, 256, 128, 8, 64, 256)
        key = jax.random.key(seed)
        ks = jax.random.split(key, 24)
        s = 0.02
        inp = {}
        inp['x'] = jax.random.normal(ks[0], (B, T, D), jnp.float32)
        flat = jnp.arange(M, dtype=jnp.int32) * 2
        inp['index_b'] = flat // T
        inp['index_t'] = flat % T
        inp['sw1'] = jax.random.normal(ks[1], (H, D), jnp.float32) * s
        inp['sb1'] = jnp.zeros((H,), jnp.float32)
        inp['sw2'] = jax.random.normal(ks[2], (H, D), jnp.float32) * s
        inp['sb2'] = jnp.zeros((H,), jnp.float32)
        inp['sw3'] = jax.random.normal(ks[3], (D, H), jnp.float32) * s
        inp['sb3'] = jnp.zeros((D,), jnp.float32)
        inp['s_ln_g'] = jnp.ones((H,), jnp.float32)
        inp['s_ln_b'] = jnp.zeros((H,), jnp.float32)
        inp['sg_w'] = jax.random.normal(ks[4], (1, D), jnp.float32) * s
        inp['sg_b'] = jnp.zeros((1,), jnp.float32)
        inp['eg_w'] = jax.random.normal(ks[5], (E, D), jnp.float32) * s
        inp['eg_b'] = jnp.zeros((E,), jnp.float32)
        inp['exp_bias'] = jnp.zeros((E,), jnp.float32)
        inp['ew1'] = jax.random.normal(ks[6], (E, H, D), jnp.float32) * s
        inp['eb1'] = jnp.zeros((E, H), jnp.float32)
        inp['ew2'] = jax.random.normal(ks[7], (E, H, D), jnp.float32) * s
        inp['eb2'] = jnp.zeros((E, H), jnp.float32)
        inp['ew3'] = jax.random.normal(ks[8], (E, D, H), jnp.float32) * s
        inp['eb3'] = jnp.zeros((E, D), jnp.float32)
        inp['sel_ln_g'] = jnp.ones((H,), jnp.float32)
        inp['sel_ln_b'] = jnp.zeros((H,), jnp.float32)
        return inp
    _L0_ffn_in = _L0_ffn_setup()

    def _L1_attn_setup():
        import jax, jax.numpy as jnp
        import numpy as np
        NUM_HEADS = 16
        PAD_ID = 0.0
        key = jax.random.key(seed)
        ks = jax.random.split(key, 9)
        B, T, C = (2, 256, 128)
        x = jax.random.normal(ks[0], (B, T, C), dtype=jnp.float32)
        lim = (6.0 / (C + C)) ** 0.5

        def w(k):
            return jax.random.uniform(k, (C, C), dtype=jnp.float32, minval=-lim, maxval=lim)

        def b(k):
            return jax.random.uniform(k, (C,), dtype=jnp.float32)
        return {'x': x, 'wq_w': w(ks[1]), 'wq_b': b(ks[2]), 'wk_w': w(ks[3]), 'wk_b': b(ks[4]), 'wv_w': w(ks[5]), 'wv_b': b(ks[6]), 'wo_w': w(ks[7]), 'wo_b': b(ks[8])}
    _L1_attn_in = _L1_attn_setup()

    def _L1_ffn_setup():
        import jax, jax.numpy as jnp
        import numpy as np
        DIM = 128

        def _reference_tuple_inner(x, W_r, W_k, W_v, mu_r, mu_k):
            B, T, C = x.shape
            x_prev = jnp.concatenate([jnp.zeros((B, 1, C), x.dtype), x[:, :-1, :]], axis=1)
            xr = mu_r * x + (1.0 - mu_r) * x_prev
            xk = mu_k * x + (1.0 - mu_k) * x_prev
            r = jax.nn.sigmoid(jnp.einsum('btc,dc->btd', xr, W_r))
            k = jnp.einsum('btc,dc->btd', xk, W_k)
            k_act = jnp.square(jax.nn.relu(k))
            out = r * jnp.einsum('btc,dc->btd', k_act, W_v)
            new_state = x[:, -1, :]
            return (out, new_state)
        key = jax.random.key(seed)
        ks = jax.random.split(key, 6)
        B, T, C = (8, 256, DIM)
        x = jax.random.normal(ks[0], (B, T, C), dtype=jnp.float32)
        s = 1.0 / np.sqrt(C)
        W_r = jax.random.uniform(ks[1], (C, C), jnp.float32, -s, s)
        W_k = jax.random.uniform(ks[2], (C, C), jnp.float32, -s, s)
        W_v = jax.random.uniform(ks[3], (C, C), jnp.float32, -s, s)
        mu_r = jax.random.uniform(ks[4], (C,), jnp.float32)
        mu_k = jax.random.uniform(ks[5], (C,), jnp.float32)
        return {'x': x, 'W_r': W_r, 'W_k': W_k, 'W_v': W_v, 'mu_r': mu_r, 'mu_k': mu_k}
    _L1_ffn_in = _L1_ffn_setup()
    _d = {'L0_attn_X': _L0_attn_in['X'], 'L0_attn_Wq': _L0_attn_in['Wq'], 'L0_attn_bq': _L0_attn_in['bq'], 'L0_attn_Wk': _L0_attn_in['Wk'], 'L0_attn_bk': _L0_attn_in['bk'], 'L0_attn_Wv': _L0_attn_in['Wv'], 'L0_attn_bv': _L0_attn_in['bv'], 'L0_attn_Wo': _L0_attn_in['Wo'], 'L0_attn_bo': _L0_attn_in['bo'], 'L0_attn_gamma': _L0_attn_in['gamma'], 'L0_attn_beta': _L0_attn_in['beta'], 'L0_attn_lam': _L0_attn_in['lam'], 'L0_ffn_index_b': _L0_ffn_in['index_b'], 'L0_ffn_index_t': _L0_ffn_in['index_t'], 'L0_ffn_sw1': _L0_ffn_in['sw1'], 'L0_ffn_sb1': _L0_ffn_in['sb1'], 'L0_ffn_sw2': _L0_ffn_in['sw2'], 'L0_ffn_sb2': _L0_ffn_in['sb2'], 'L0_ffn_sw3': _L0_ffn_in['sw3'], 'L0_ffn_sb3': _L0_ffn_in['sb3'], 'L0_ffn_s_ln_g': _L0_ffn_in['s_ln_g'], 'L0_ffn_s_ln_b': _L0_ffn_in['s_ln_b'], 'L0_ffn_sg_w': _L0_ffn_in['sg_w'], 'L0_ffn_sg_b': _L0_ffn_in['sg_b'], 'L0_ffn_eg_w': _L0_ffn_in['eg_w'], 'L0_ffn_eg_b': _L0_ffn_in['eg_b'], 'L0_ffn_exp_bias': _L0_ffn_in['exp_bias'], 'L0_ffn_ew1': _L0_ffn_in['ew1'], 'L0_ffn_eb1': _L0_ffn_in['eb1'], 'L0_ffn_ew2': _L0_ffn_in['ew2'], 'L0_ffn_eb2': _L0_ffn_in['eb2'], 'L0_ffn_ew3': _L0_ffn_in['ew3'], 'L0_ffn_eb3': _L0_ffn_in['eb3'], 'L0_ffn_sel_ln_g': _L0_ffn_in['sel_ln_g'], 'L0_ffn_sel_ln_b': _L0_ffn_in['sel_ln_b'], 'L1_attn_wq_w': _L1_attn_in['wq_w'], 'L1_attn_wq_b': _L1_attn_in['wq_b'], 'L1_attn_wk_w': _L1_attn_in['wk_w'], 'L1_attn_wk_b': _L1_attn_in['wk_b'], 'L1_attn_wv_w': _L1_attn_in['wv_w'], 'L1_attn_wv_b': _L1_attn_in['wv_b'], 'L1_attn_wo_w': _L1_attn_in['wo_w'], 'L1_attn_wo_b': _L1_attn_in['wo_b'], 'L1_ffn_W_r': _L1_ffn_in['W_r'], 'L1_ffn_W_k': _L1_ffn_in['W_k'], 'L1_ffn_W_v': _L1_ffn_in['W_v'], 'L1_ffn_mu_r': _L1_ffn_in['mu_r'], 'L1_ffn_mu_k': _L1_ffn_in['mu_k']}
    _x0 = _d['L0_attn_X']
    _d['L0_attn_X'] = jax.random.normal(jax.random.fold_in(jax.random.key(seed), 1), (2, 1024, 128), dtype=_x0.dtype)
    del _x0
    return _d

def reference(L0_attn_X, L0_attn_Wq, L0_attn_bq, L0_attn_Wk, L0_attn_bk, L0_attn_Wv, L0_attn_bv, L0_attn_Wo, L0_attn_bo, L0_attn_gamma, L0_attn_beta, L0_attn_lam, L0_ffn_index_b, L0_ffn_index_t, L0_ffn_sw1, L0_ffn_sb1, L0_ffn_sw2, L0_ffn_sb2, L0_ffn_sw3, L0_ffn_sb3, L0_ffn_s_ln_g, L0_ffn_s_ln_b, L0_ffn_sg_w, L0_ffn_sg_b, L0_ffn_eg_w, L0_ffn_eg_b, L0_ffn_exp_bias, L0_ffn_ew1, L0_ffn_eb1, L0_ffn_ew2, L0_ffn_eb2, L0_ffn_ew3, L0_ffn_eb3, L0_ffn_sel_ln_g, L0_ffn_sel_ln_b, L1_attn_wq_w, L1_attn_wq_b, L1_attn_wk_w, L1_attn_wk_b, L1_attn_wv_w, L1_attn_wv_b, L1_attn_wo_w, L1_attn_wo_b, L1_ffn_W_r, L1_ffn_W_k, L1_ffn_W_v, L1_ffn_mu_r, L1_ffn_mu_k):

    def _L0_attn_ref(X, Wq, bq, Wk, bk, Wv, bv, Wo, bo, gamma, beta, lam):
        import jax, jax.numpy as jnp
        import numpy as np
        B, S, E, H, D = (1, 256, 128, 16, 64)
        LAM_INIT = 0.8
        LN_EPS = 1e-05
        Q = jnp.einsum('bse,hec->bhsc', X, Wq) + bq[None, :, None, :]
        K = jnp.einsum('bse,hec->bhsc', X, Wk) + bk[None, :, None, :]
        V = jnp.einsum('bse,hed->bhsd', X, Wv) + bv[None, :, None, :]
        d = Wv.shape[-1]
        Q1, Q2 = (Q[..., :d], Q[..., d:])
        K1, K2 = (K[..., :d], K[..., d:])
        s = 1.0 / jnp.sqrt(jnp.float32(d))
        A1 = jnp.einsum('bhqd,bhkd->bhqk', Q1, K1) * s
        A2 = jnp.einsum('bhqd,bhkd->bhqk', Q2, K2) * s
        P = jax.nn.softmax(A1, axis=-1) - lam * jax.nn.softmax(A2, axis=-1)
        O = jnp.einsum('bhqk,bhkd->bhqd', P, V)
        Ocat = jnp.transpose(O, (0, 2, 1, 3)).reshape(O.shape[0], O.shape[2], -1)
        Y = Ocat @ Wo + bo
        mu = jnp.mean(Y, axis=-1, keepdims=True)
        var = jnp.var(Y, axis=-1, keepdims=True)
        Yn = (Y - mu) * jax.lax.rsqrt(var + LN_EPS) * gamma + beta
        return Yn * (1.0 - LAM_INIT)

    def _L0_ffn_ref(x, index_b, index_t, sw1, sb1, sw2, sb2, sw3, sb3, s_ln_g, s_ln_b, sg_w, sg_b, eg_w, eg_b, exp_bias, ew1, eb1, ew2, eb2, ew3, eb3, sel_ln_g, sel_ln_b):
        import jax, jax.numpy as jnp
        import numpy as np
        EPS = 1e-05

        def _ln(x, g, b):
            mu = jnp.mean(x, axis=-1, keepdims=True)
            var = jnp.mean(jnp.square(x - mu), axis=-1, keepdims=True)
            return (x - mu) * jax.lax.rsqrt(var + EPS) * g + b

        def _forward(x, index_b, index_t, sw1, sb1, sw2, sb2, sw3, sb3, s_ln_g, s_ln_b, sg_w, sg_b, eg_w, eg_b, exp_bias, ew1, eb1, ew2, eb2, ew3, eb3, sel_ln_g, sel_ln_b):
            x1 = jnp.einsum('btd,hd->bth', x, sw1) + sb1
            x2 = jnp.einsum('btd,hd->bth', x, sw2) + sb2
            sh = _ln(jax.nn.silu(x1) * x2, s_ln_g, s_ln_b)
            shared_out = jnp.einsum('bth,dh->btd', sh, sw3) + sb3
            x_moe = x[index_b, index_t]
            shared_scores = jax.nn.sigmoid(x_moe @ sg_w.T + sg_b)
            expert_scores = jax.nn.sigmoid(x_moe @ eg_w.T + eg_b)
            top1_idx = jnp.argmax(expert_scores + exp_bias, axis=-1)
            top1_score = jnp.take_along_axis(expert_scores, top1_idx[:, None], axis=-1)
            weights = jax.nn.softmax(jnp.concatenate([shared_scores, top1_score], axis=-1), axis=-1)
            shared_w, expert_w = (weights[:, 0], weights[:, 1])
            shared_moe_out = shared_out[index_b, index_t] * shared_w[:, None]
            h1 = jnp.einsum('md,ehd->meh', x_moe, ew1) + eb1
            h2 = jnp.einsum('md,ehd->meh', x_moe, ew2) + eb2
            z = _ln(jax.nn.silu(h1) * h2, sel_ln_g, sel_ln_b)
            out_all = jnp.einsum('meh,edh->med', z, ew3) + eb3
            expert_out = jnp.take_along_axis(out_all, top1_idx[:, None, None], axis=1)[:, 0]
            expert_moe_out = expert_out * expert_w[:, None]
            final_out = shared_out.at[index_b, index_t].set(shared_moe_out + expert_moe_out)
            return final_out
        return _forward(x, index_b, index_t, sw1, sb1, sw2, sb2, sw3, sb3, s_ln_g, s_ln_b, sg_w, sg_b, eg_w, eg_b, exp_bias, ew1, eb1, ew2, eb2, ew3, eb3, sel_ln_g, sel_ln_b)

    def _L1_attn_ref(x, wq_w, wq_b, wk_w, wk_b, wv_w, wv_b, wo_w, wo_b):
        import jax, jax.numpy as jnp
        import numpy as np
        NUM_HEADS = 16
        PAD_ID = 0.0
        B, T, C = x.shape
        H = NUM_HEADS
        Dh = C // H
        scale = Dh ** (-0.5)
        q = (x @ wq_w.T + wq_b).reshape(B, T, H, Dh)
        k = (x @ wk_w.T + wk_b).reshape(B, T, H, Dh)
        v = (x @ wv_w.T + wv_b).reshape(B, T, H, Dh)
        scores = jnp.einsum('bthd,bshd->bhts', q, k) * scale
        key_mask = (x[:, :, 0] != PAD_ID)[:, None, None, :]
        scores = jnp.where(key_mask, scores, -jnp.inf)
        attn = jax.nn.softmax(scores, axis=-1)
        out = jnp.einsum('bhts,bshd->bthd', attn, v).reshape(B, T, C)
        return out @ wo_w.T + wo_b

    def _L1_ffn_ref(x, W_r, W_k, W_v, mu_r, mu_k):
        import jax, jax.numpy as jnp
        import numpy as np
        DIM = 128

        def _reference_tuple_inner(x, W_r, W_k, W_v, mu_r, mu_k):
            B, T, C = x.shape
            x_prev = jnp.concatenate([jnp.zeros((B, 1, C), x.dtype), x[:, :-1, :]], axis=1)
            xr = mu_r * x + (1.0 - mu_r) * x_prev
            xk = mu_k * x + (1.0 - mu_k) * x_prev
            r = jax.nn.sigmoid(jnp.einsum('btc,dc->btd', xr, W_r))
            k = jnp.einsum('btc,dc->btd', xk, W_k)
            k_act = jnp.square(jax.nn.relu(k))
            out = r * jnp.einsum('btc,dc->btd', k_act, W_v)
            new_state = x[:, -1, :]
            return (out, new_state)
        return _reference_tuple_inner(x, W_r, W_k, W_v, mu_r, mu_k)[0]
    x = L0_attn_X
    x = x + _L0_attn_ref(_layernorm(x, axis=-1), L0_attn_Wq, L0_attn_bq, L0_attn_Wk, L0_attn_bk, L0_attn_Wv, L0_attn_bv, L0_attn_Wo, L0_attn_bo, L0_attn_gamma, L0_attn_beta, L0_attn_lam)
    x = x + _L0_ffn_ref(_layernorm(x, axis=-1), L0_ffn_index_b, L0_ffn_index_t, L0_ffn_sw1, L0_ffn_sb1, L0_ffn_sw2, L0_ffn_sb2, L0_ffn_sw3, L0_ffn_sb3, L0_ffn_s_ln_g, L0_ffn_s_ln_b, L0_ffn_sg_w, L0_ffn_sg_b, L0_ffn_eg_w, L0_ffn_eg_b, L0_ffn_exp_bias, L0_ffn_ew1, L0_ffn_eb1, L0_ffn_ew2, L0_ffn_eb2, L0_ffn_ew3, L0_ffn_eb3, L0_ffn_sel_ln_g, L0_ffn_sel_ln_b)
    x = x + _L1_attn_ref(_layernorm(x, axis=-1), L1_attn_wq_w, L1_attn_wq_b, L1_attn_wk_w, L1_attn_wk_b, L1_attn_wv_w, L1_attn_wv_b, L1_attn_wo_w, L1_attn_wo_b)
    x = x + _L1_ffn_ref(_layernorm(x, axis=-1), L1_ffn_W_r, L1_ffn_W_k, L1_ffn_W_v, L1_ffn_mu_r, L1_ffn_mu_k)
    return x

_drawn_inputs = setup_inputs


def setup_inputs(seed=0):
    import zlib

    import numpy as np

    out = dict(_drawn_inputs(seed))
    spreads = {'L0_attn_bq': (0.0, 0.8),
     'L0_attn_bk': (0.0, 2.0),
     'L0_attn_bv': (0.0, 0.462),
     'L0_attn_bo': (0.0, 0.1),
     'L0_attn_gamma': (1.0, 0.2),
     'L0_attn_beta': (0.0, 0.432),
     'L0_ffn_sb1': (0.0, 0.1),
     'L0_ffn_sb2': (0.0, 0.1),
     'L0_ffn_sb3': (0.0, 0.1),
     'L0_ffn_s_ln_g': (1.0, 0.6),
     'L0_ffn_s_ln_b': (0.0, 0.501),
     'L0_ffn_eg_b': (0.0, 0.8),
     'L0_ffn_exp_bias': (0.0, 0.1),
     'L0_ffn_eb1': (0.0, 2.0),
     'L0_ffn_eb2': (0.0, 2.0),
     'L0_ffn_eb3': (0.0, 0.665),
     'L0_ffn_sel_ln_g': (1.0, 0.6),
     'L0_ffn_sel_ln_b': (0.0, 2.0)}
    factors = {'L0_attn_Wq': 8.0,
     'L0_attn_Wk': 8.0,
     'L0_attn_Wv': 8.0,
     'L0_ffn_sg_w': 102.699,
     'L0_ffn_eg_w': 4.319,
     'L0_ffn_ew1': 13.322,
     'L0_ffn_ew2': 12.33,
     'L1_attn_wk_b': 200.0,
     'L1_ffn_W_r': 3.852,
     'L1_ffn_mu_r': 8.0}
    for name, (base, spread) in spreads.items():
        noise = np.random.default_rng([zlib.crc32(name.encode()), seed]).standard_normal(out[name].shape)
        drawn = base * np.exp(spread * noise) if base else spread * noise
        out[name] = jnp.asarray(drawn.astype(out[name].dtype))
    for name, factor in factors.items():
        out[name] = (out[name] * factor).astype(out[name].dtype)
    return out
```

```python
import concourse.bass as bass
from concourse import mybir
from contextlib import ExitStack

F32 = mybir.dt.float32
F16 = mybir.dt.float16
I32 = mybir.dt.int32
ALU = mybir.AluOpType
ACT = mybir.ActivationFunctionType
AX = mybir.AxisListType

B, T, E = 2, 1024, 128
NT = T // 128
TT = B * NT
N = B * T
HF = 512
H0, D0 = 16, 64
H1, D1 = 16, 8
G1 = 4
NX, HE = 8, 64
M = 256
EPS = 1e-5
OUT_SCALE = 1.0 - 0.8
SCALE0 = 1.0 / D0 ** 0.5
SCALE1 = float(D1) ** -0.5
MASKED = -60000.0


def two_layers(nc, a, out):
    ctx = ExitStack()
    with ctx:
        def sb(name, shape, dt=F32):
            return ctx.enter_context(nc.sbuf_tensor(name, shape, dt))

        def sem(name):
            return ctx.enter_context(nc.semaphore(name))

        PS = ctx.enter_context(nc.psum_tensor("PS", [128, 8, 512], F32))
        MX, OT, MISC = PS[:, 4:6, :], PS[:, 6, :], PS[:, 7, :]

        x = sb("x", [128, TT, E])
        xT = sb("xT", [128, N])
        t1 = sb("t1", [128, TT, E])
        t2 = sb("t2", [128, TT, E])
        t3 = sb("t3", [128, TT, E])
        yT = sb("yT", [128, N])
        ering = sb("ering", [128, 8, 2, HF])
        eflat = ering[:, :, :, :].rearrange("p a b c -> p (a b c)")
        acc = sb("acc", [128, 2, 2, HF])
        region = sb("region", [128, 24576], F16)
        vslot = sb("vslot", [128, 2, NT, D0])
        osb = sb("osb", [128, HF])
        rcp = sb("rcp", [128, HF])
        on = sb("on", [128, HF])
        wq_s = sb("wq_s", [128, 128])
        wk_s = sb("wk_s", [128, 128])
        wv_s = sb("wv_s", [128, D0])
        wo_raw = sb("wo_raw", [128, E])
        wo_s = sb("wo_s", [128, E])
        ident = sb("ident", [128, 128])
        ident16 = sb("ident16", [128, 128], F16)
        ones = sb("ones", [128, 64])
        wt = sb("wt", [128, 8, 128])
        SW12T, WQT, WKT, WVT, WOT, WRT, WCT, WVV = range(8)
        ew1T = sb("ew1T", [128, NX * HE])
        ew2T = sb("ew2T", [128, NX * HE])
        ew3T = sb("ew3T", [HE, NX, E])
        small = sb("small", [128, 320])
        sw3T, gwT = small[0:HE, 0:128], small[:, 128:137]
        bqk = small[:, 256:288].rearrange("p (h i) -> p h i", i=2)
        bv_b = sb("bv_b", [128, H0 * D0])
        gam_b = sb("gam_b", [128, E])
        bet_b = sb("bet_b", [128, E])
        sb12_b = sb("sb12_b", [128, 2 * HE])
        sb3_b = sb("sb3_b", [128, E])
        eb1_b = sb("eb1_b", [128, NX * HE])
        eb2_b = sb("eb2_b", [128, NX * HE])
        selg_b = sb("selg_b", [128, HE])
        selb_b = sb("selb_b", [128, HE])
        xb_b = sb("xb_b", [128, NX])
        gb_b = sb("gb_b", [128, 1 + NX])
        wvb_b = sb("wvb_b", [128, E])
        eb3 = sb("eb3", [NX, E])
        cols = sb("cols", [128, 16])
        BO, WOB, MUR, MUK, SLG, SLB, LAM, ZERO, PIDX, OMR, OMK = range(11)
        ib_b = sb("ib_b", [128, 2, M], I32)
        icol = sb("icol", [128, 2, 2], I32)
        fb = sb("fb", [128, M])
        fcol = sb("fcol", [128, 2])
        mxp = sb("mxp", [128, 2, 32])
        cm = sb("cm", [128, 16])
        c16 = sb("c16", [128, 32], F16)
        cts = sb("cts", [8, HF], F16)
        st6 = sb("st6", [128, TT, 6])
        mv = sb("mv", [128, TT, 2])
        bcur = sb("bcur", [128, 2])
        rstd = sb("rstd", [128, TT])
        var = sb("var", [128, 2, TT])
        row = sb("row", [1, 10, 128])
        pcol = sb("pcol", [128, 10])
        bias1 = sb("bias1", [1, 2, 128])
        wqa = sb("wqa", [128, 2, G1, 128])
        wo1 = sb("wo1", [128, G1, E])
        sel = sb("sel", [128, 128])
        mrow = sb("mrow", [1, N], F16)
        kmask = sb("kmask", [128, TT])
        va = sb("va", [128, TT, E])
        gt = sb("gt", [128, 2, 48])

        def flat(t):
            return t[:, :, :].rearrange("p a b -> p (a b)")

        def r16(lo, n):
            return region[:, lo:lo + n]

        nat = [r16(i * 2048, 2048).rearrange("p (b t) -> p b t", b=2) for i in range(4)]
        QH, QL, KH, KL = nat
        asm = [r16(8192 + i * 4096, 4096).rearrange("p (b s t) -> p b s t", b=2, s=2) for i in range(4)]
        QA, QB, KA, KB = asm
        QN = r16(0, 8192).rearrange("p (g t) -> p g t", g=G1)
        KN = r16(8192, 8192).rearrange("p (g t) -> p g t", g=G1)
        slots = [r16(16384 + i * 2048, 2048).rearrange("p (b t) -> p b t", b=2) for i in range(2)]
        KM, QS = slots
        QM, KS = [[t[:, :].bitcast(F16).rearrange("p (j t) -> p j t", j=4) for t in pair]
                  for pair in ((flat(t1), flat(t2)), (flat(t3), xT))]
        vst = acc[:, :, :, :].rearrange("p b s t -> p b (s t)").rearrange(
            "p b (k j c) -> p b k j c", k=NT, j=G1)

        s_ld_x = sem("s_ld_x")
        s_ld_w = sem("s_ld_w")
        s_ld_c = sem("s_ld_c")
        s_ld_wqk = sem("s_ld_wqk")
        s_ld_wv = sem("s_ld_wv")
        s_ld_wo = sem("s_ld_wo")
        s_ident_ok = sem("s_ident_ok")
        s_ones_ok = sem("s_ones_ok")
        s_dve_chain = sem("s_dve_chain")
        s_pool_chain = sem("s_pool_chain")
        s_wprep_mm = sem("s_wprep_mm")
        s_wprep_ev = sem("s_wprep_ev")
        s_xn_ok = sem("s_xn_ok")
        s_xt_mm = sem("s_xt_mm")
        s_xt_ev = sem("s_xt_ev")
        s_kb_ok = sem("s_kb_ok")
        s_yinit = sem("s_yinit")
        s_lam_ok = sem("s_lam_ok")
        s_scores = sem("s_scores")
        s_exps = sem("s_exps")
        s_pv = sem("s_pv")
        s_accs = sem("s_accs")
        s_sums = sem("s_sums")
        s_maxmm = sem("s_maxmm")
        s_maxed = sem("s_maxed")
        s_cmax = sem("s_cmax")
        s_chi = sem("s_chi")
        s_c_ok = sem("s_c_ok")
        s_ct_mm = sem("s_ct_mm")
        s_ct_ev = sem("s_ct_ev")
        s_c_dma = sem("s_c_dma")
        s_asm_dma = sem("s_asm_dma")
        s_qk_mm = sem("s_qk_mm")
        s_hi_ok = sem("s_hi_ok")
        s_lo_ok = sem("s_lo_ok")
        s_v_mm = sem("s_v_mm")
        s_v_ev = sem("s_v_ev")
        s_os_ok = sem("s_os_ok")
        s_rc_ok = sem("s_rc_ok")
        s_on_ok = sem("s_on_ok")
        s_y_mm = sem("s_y_mm")
        s_y_ok = sem("s_y_ok")
        s_wo_ok = sem("s_wo_ok")
        s_yt_mm = sem("s_yt_mm")
        s_x2_ok = sem("s_x2_ok")
        s_x2t_mm = sem("s_x2t_mm")
        s_x2t_ev = sem("s_x2t_ev")
        s_h_mm = sem("s_h_mm")
        s_h_ev = sem("s_h_ev")
        s_z_ok = sem("s_z_ok")
        s_zt_mm = sem("s_zt_mm")
        s_zt_ev = sem("s_zt_ev")
        s_sh_mm = sem("s_sh_mm")
        s_sh_ev = sem("s_sh_ev")
        s_g_ok = sem("s_g_ok")
        s_gat_mm = sem("s_gat_mm")
        s_gat_ev = sem("s_gat_ev")
        s_m_mm = sem("s_m_mm")
        s_act_a = sem("s_act_a")
        s_act_b = sem("s_act_b")
        s_zs_ok = sem("s_zs_ok")
        s_zst_mm = sem("s_zst_mm")
        s_zst_ev = sem("s_zst_ev")
        s_eo_mm = sem("s_eo_mm")
        s_eo_ok = sem("s_eo_ok")
        s_sc_mm = sem("s_sc_mm")
        s_x3_ok = sem("s_x3_ok")
        s_x3t_mm = sem("s_x3t_mm")
        s_x3t_ev = sem("s_x3t_ev")
        s_b1_ok = sem("s_b1_ok")
        s_b1_mm = sem("s_b1_mm")
        s_b1_ev = sem("s_b1_ev")
        s_wqa_ok = sem("s_wqa_ok")
        s_v1_mm = sem("s_v1_mm")
        s_v1_ev = sem("s_v1_ev")
        s_p1_mm = sem("s_p1_mm")
        s_p1_x = sem("s_p1_x")
        s_p1_ok = sem("s_p1_ok")
        s_mr_ok = sem("s_mr_ok")
        s_zero_ok = sem("s_zero_ok")
        s_mr_dma = sem("s_mr_dma")
        s_msk_ok = sem("s_msk_ok")
        s_scores1 = sem("s_scores1")
        s_exps1 = sem("s_exps1")
        s_pv1 = sem("s_pv1")
        s_max1 = sem("s_max1")
        s_maxed1 = sem("s_maxed1")
        s_cmax1 = sem("s_cmax1")
        s_chi1 = sem("s_chi1")
        s_c_ok1 = sem("s_c_ok1")
        s_ct_mm1 = sem("s_ct_mm1")
        s_ct_ev1 = sem("s_ct_ev1")
        s_c_dma1 = sem("s_c_dma1")
        s_stm_dma = sem("s_stm_dma")
        s_sts_dma = sem("s_sts_dma")
        s_stv_ok = sem("s_stv_ok")
        s_sto_dma = sem("s_sto_dma")
        s_os1_ok = sem("s_os1_ok")
        s_sel_mm = sem("s_sel_mm")
        s_tot1_ok = sem("s_tot1_ok")
        s_rc1_ok = sem("s_rc1_ok")
        s_on1_ok = sem("s_on1_ok")
        s_y1_mm = sem("s_y1_mm")
        s_y1_ok = sem("s_y1_ok")
        s_bc_ok = sem("s_bc_ok")
        s_var_ok = sem("s_var_ok")
        s_root_ok = sem("s_root_ok")
        s_k2_ok = sem("s_k2_ok")
        s_wo1_dma = sem("s_wo1_dma")
        s_z1t_mm = sem("s_z1t_mm")
        s_x4_ok = sem("s_x4_ok")
        s_x4t_mm = sem("s_x4t_mm")
        s_x4t_ev = sem("s_x4t_ev")
        s_xr_ok = sem("s_xr_ok")
        s_k_mm = sem("s_k_mm")
        s_k_ev = sem("s_k_ev")
        s_r_mm = sem("s_r_mm")
        s_r_ev = sem("s_r_ev")
        s_o_mm = sem("s_o_mm")
        s_o_ok = sem("s_o_ok")
        s_out_dma = sem("s_out_dma")
        s_gate_a = sem("s_gate_a")
        s_gate_b = sem("s_gate_b")

        def upto(count):
            return max(count, 0) if isinstance(count, int) else count

        def chained(eng, done):
            count = [0]

            def link(ins):
                count[0] += 1
                ins.then_inc(done, 1)
                eng.wait_ge(done, count[0])
            return link

        block = ctx.enter_context(nc.Block())
        last0 = 2 * H0

        def heads(eng, item):
            for b in range(2):
                item(-1, b)
            for b in range(2):
                item(0, b)
            with eng.Fori(1, H0 - 1) as h:
                for b in range(2):
                    item(h, b)
            for b in range(2):
                item(H0 - 1, b)

        def flags(h, b):
            if isinstance(h, int):
                n = 2 * h + b
                return 0 <= n < last0, 0 <= n + 1 < last0, 0 <= n + 2 < last0
            return True, True, True

        def groups(eng, item):
            for b in range(2):
                item(-1, b)
            for b in range(2):
                item(0, b)
            with eng.Fori(1, G1 - 1) as g:
                for b in range(2):
                    item(g, b)
            for b in range(2):
                item(G1 - 1, b)

        def flags1(g, b):
            if isinstance(g, int):
                n = 2 * g + b
                return 0 <= n < 2 * G1, 0 <= n + 1 < 2 * G1, 0 <= n + 2 < 2 * G1
            return True, True, True

        def bc(name, n):
            return a[name].rearrange("(o n) -> o n", o=1).to_broadcast([128, n])

        def glu(t):
            return t[:, :, 0:HE], t[:, :, HE:2 * HE]

        @block.sync
        def _(sp):
            xv = a["L0_attn_X"].rearrange("b (k p) e -> p (b k) e", p=128)
            for i in range(4):
                sp.dma_start(x[:, 4 * i:4 * i + 4, :], xv[:, 4 * i:4 * i + 4, :]).then_inc(s_ld_x, 16)
            sp.dma_start(eflat[0:16, 2900:3028], a["L0_attn_bq"]).then_inc(s_ld_w, 16)
            sp.dma_start(eflat[0:16, 3028:3156], a["L0_attn_bk"]).then_inc(s_ld_w, 16)
            sp.dma_start(wq_s[:, :], a["L0_attn_Wq"][0]).then_inc(s_ld_wqk, 16)
            sp.dma_start(wk_s[:, :], a["L0_attn_Wk"][0]).then_inc(s_ld_wqk, 16)
            sp.dma_start(wv_s[:, :], a["L0_attn_Wv"][0]).then_inc(s_ld_wv, 16)
            for k in range(2):
                sp.dma_start(wo_raw[64 * k:64 * k + 64, :], a["L0_attn_Wo"][0:D0, :]).then_inc(s_ld_wo, 16)

            def raw(i):
                return eflat[:, 128 * i:128 * i + 128]
            sp.dma_start(raw(0)[0:64, :], a["L0_ffn_sw1"]).then_inc(s_ld_w, 16)
            sp.dma_start(raw(0)[64:128, :], a["L0_ffn_sw2"]).then_inc(s_ld_w, 16)
            for i, nme in enumerate(("L1_attn_wq_w", "L1_attn_wk_w", "L1_attn_wv_w", "L1_attn_wo_w",
                                     "L1_ffn_W_r", "L1_ffn_W_k", "L1_ffn_W_v")):
                sp.dma_start(raw(1 + i), a[nme]).then_inc(s_ld_w, 16)
            sp.dma_start(raw(8)[0:1, :], a["L0_ffn_sg_w"]).then_inc(s_ld_w, 16)
            sp.dma_start(raw(8)[1:9, :], a["L0_ffn_eg_w"]).then_inc(s_ld_w, 16)
            for i, nme in ((9, "L0_ffn_ew1"), (13, "L0_ffn_ew2")):
                sp.dma_start(eflat[:, 128 * i:128 * i + 512].rearrange("p (k d) -> p k d", k=4), a[nme].rearrange("(k e) h d -> (e h) k d", k=4)).then_inc(s_ld_w, 16)
            sp.dma_start(eflat[:, 2304:2816].rearrange("p (e h) -> p e h", e=NX), a["L0_ffn_ew3"].rearrange("e d h -> d e h")).then_inc(s_ld_w, 16)
            sp.dma_start(eflat[:, 2816:2880], a["L0_ffn_sw3"]).then_inc(s_ld_w, 16)

            def col(i, nme, n=128, lo=0):
                sp.dma_start(cols[lo:lo + n, i:i + 1], a[nme].rearrange("(p o) -> p o", o=1)).then_inc(s_ld_c, 16)
            col(BO, "L0_attn_bo")
            col(WOB, "L1_attn_wo_b")
            col(MUR, "L1_ffn_mu_r")
            col(MUK, "L1_ffn_mu_k")
            col(SLG, "L0_ffn_s_ln_g", HE)
            col(SLB, "L0_ffn_s_ln_b", HE)
            sp.dma_start(cols[64:128, LAM:LAM + 1], a["L0_attn_lam"].rearrange("(o n) -> o n", o=1).to_broadcast([64, 1])).then_inc(s_ld_c, 16)
            sp.dma_start(bv_b[:, :], a["L0_attn_bv"].rearrange("h (o d) -> o (h d)", o=1).to_broadcast([128, H0 * D0])).then_inc(s_ld_c, 16)
            sp.dma_start(gam_b[:, :], bc("L0_attn_gamma", E)).then_inc(s_ld_c, 16)
            sp.dma_start(bet_b[:, :], bc("L0_attn_beta", E)).then_inc(s_ld_c, 16)
            sp.dma_start(sb12_b[:, 0:HE], bc("L0_ffn_sb1", HE)).then_inc(s_ld_c, 16)
            sp.dma_start(sb12_b[:, HE:2 * HE], bc("L0_ffn_sb2", HE)).then_inc(s_ld_c, 16)
            sp.dma_start(sb3_b[:, :], bc("L0_ffn_sb3", E)).then_inc(s_ld_c, 16)
            sp.dma_start(eb1_b[:, :], a["L0_ffn_eb1"].rearrange("e (o h) -> o (e h)", o=1).to_broadcast([128, NX * HE])).then_inc(s_ld_c, 16)
            sp.dma_start(eb2_b[:, :], a["L0_ffn_eb2"].rearrange("e (o h) -> o (e h)", o=1).to_broadcast([128, NX * HE])).then_inc(s_ld_c, 16)
            sp.dma_start(selg_b[:, :], bc("L0_ffn_sel_ln_g", HE)).then_inc(s_ld_c, 16)
            sp.dma_start(selb_b[:, :], bc("L0_ffn_sel_ln_b", HE)).then_inc(s_ld_c, 16)
            sp.dma_start(xb_b[:, :], bc("L0_ffn_exp_bias", NX)).then_inc(s_ld_c, 16)
            sp.dma_start(gb_b[:, 0:1], bc("L0_ffn_sg_b", 1)).then_inc(s_ld_c, 16)
            sp.dma_start(gb_b[:, 1:9], bc("L0_ffn_eg_b", NX)).then_inc(s_ld_c, 16)
            sp.dma_start(wvb_b[:, :], bc("L1_attn_wv_b", E)).then_inc(s_ld_c, 16)
            sp.dma_start(eb3[:, :], a["L0_ffn_eb3"]).then_inc(s_ld_c, 16)
            sp.dma_start(ib_b[:, 0, :], bc("L0_ffn_index_b", M)).then_inc(s_ld_c, 16)
            sp.dma_start(ib_b[:, 1, :], bc("L0_ffn_index_t", M)).then_inc(s_ld_c, 16)
            for i, nme in enumerate(("L0_ffn_index_b", "L0_ffn_index_t")):
                for k in range(2):
                    sp.dma_start(icol[:, i, k:k + 1], a[nme][k * 128:k * 128 + 128].rearrange("(p o) -> p o", o=1)).then_inc(s_ld_c, 16)
            sp.dma_start(bias1[0:1, 0, :], a["L1_attn_wq_b"].rearrange("(o n) -> o n", o=1)).then_inc(s_ld_c, 16)
            sp.dma_start(bias1[0:1, 1, :], a["L1_attn_wk_b"].rearrange("(o n) -> o n", o=1)).then_inc(s_ld_c, 16)

            def c_rows(h, b, qh):
                m = 2 * h + b
                sp.wait_ge(s_ct_ev, upto(2 * m + qh + 1))
                for part in range(2):
                    sp.dma_start(QB[64:66, b, part, qh * HF:qh * HF + HF], cts[2 * part:2 * part + 2, :]).then_inc(s_c_dma, 16)

            def item(h, b):
                own, nxt, prj = flags(h, b)
                n = 2 * h + b
                p1 = 1 - b
                if b == 0 and own and prj:
                    sp.wait_ge(s_qk_mm, upto(4 * (n + 2)))
                    sp.dma_start(wq_s[:, :], a["L0_attn_Wq"][bass.ds(h + 1, 1)].rearrange("o e c -> (o e) c")).then_inc(s_ld_wqk, 16)
                    sp.dma_start(wk_s[:, :], a["L0_attn_Wk"][bass.ds(h + 1, 1)].rearrange("o e c -> (o e) c")).then_inc(s_ld_wqk, 16)
                if nxt:
                    sp.wait_ge(s_maxmm, upto(16 * (n + 1) + 1))
                    for part in range(2):
                        src = slice(64 * part, 64 * part + 64)
                        for dst, at, frm in ((QA, 0, QH), (QA, 64, QH), (QB, 0, QL), (KA, 0, KH), (KA, 64, KL),
                                             (KB, 0, KH)):
                            sp.dma_start(dst[at:at + 64, p1, part, :], frm[src, p1, :]).then_inc(s_asm_dma, 16)
                if own:
                    c_rows(h, b, 1)
                if nxt:
                    c_rows(h + b, p1, 0)
                if b == 0 and (not isinstance(h, int) or 0 <= h < H0 - 1):
                    sp.wait_ge(s_v_mm, upto(n + 2))
                    sp.dma_start(wv_s[:, :], a["L0_attn_Wv"][bass.ds(h + 1, 1)].rearrange("o e c -> (o e) c")).then_inc(s_ld_wv, 16)
                    sp.wait_ge(s_wo_ok, upto(h + 1))
                    for k in range(2):
                        sp.dma_start(wo_raw[64 * k:64 * k + 64, :], a["L0_attn_Wo"][bass.ds((h + 1) * D0, D0), :]).then_inc(s_ld_wo, 16)

            heads(sp, item)

            sp.wait_ge(s_p1_ok, 32)
            sp.wait_ge(s_mr_ok, 1)
            for g in range(G1):
                for j in range(4):
                    sp.dma_start(KN[32 * j + 24:32 * j + 25, g, :], mrow[0:1, :]).then_inc(s_mr_dma, 16)
            sp.wait_ge(s_mr_dma, 16 * 16)
            sp.wait_ge(s_wprep_ev, 3)
            sp.wait_ge(s_b1_ok, 2)
            for g in range(G1):
                for j in range(4):
                    sp.dma_start(wo1[32 * j:32 * j + 8, g, :], wt[32 * g + 8 * j:32 * g + 8 * j + 8, WOT, :]).then_inc(s_wo1_dma, 16)
            sp.wait_ge(s_wo1_dma, 16 * 16)

            def c_rows1(g, b, qh):
                n = 2 * g + b
                sp.wait_ge(s_ct_ev1, upto(2 * n + qh + 1))
                for j in range(4):
                    sp.dma_start(QS[32 * j + 25:32 * j + 27, b, qh * HF:qh * HF + HF], cts[2 * j:2 * j + 2, :]).then_inc(s_c_dma1, 16)

            def item1(g, b):
                own, nxt, prj = flags1(g, b)
                n = 2 * g + b
                p1 = 1 - b
                if nxt:
                    sp.wait_ge(s_scores1, upto(32 * n))
                    gn = g + b
                    sp.dma_start(QS[:, p1, :], QN[:, bass.ds(gn, 1), p1 * T:p1 * T + T].rearrange(
                        "p o t -> p (o t)")).then_inc(s_sts_dma, 16)
                    for j in range(4):
                        at = slice(32 * j, 32 * j + 32)
                        sp.dma_start(KS[p1][at, j, :], KN[at, bass.ds(gn, 1), p1 * T:p1 * T + T].rearrange(
                            "p o t -> p (o t)")).then_inc(s_sts_dma, 16)
                if own:
                    c_rows1(g, b, 1)
                if prj:
                    if not isinstance(g, int) or n >= -1:
                        sp.wait_ge(s_max1, upto(64 * (n + 1) + 1))
                    sp.dma_start(KM[:, b, :], KN[:, bass.ds(g + 1, 1), b * T:b * T + T].rearrange(
                        "p o t -> p (o t)")).then_inc(s_stm_dma, 16)
                    for j in range(4):
                        at = slice(32 * j, 32 * j + 32)
                        sp.dma_start(QM[b][at, j, :], QN[at, bass.ds(g + 1, 1), b * T:b * T + T].rearrange(
                            "p o t -> p (o t)")).then_inc(s_stm_dma, 16)
                if b == 0 and own:
                    sp.wait_ge(s_y1_mm, upto(2 * n))
                    sp.dma_start(wo_s[:, :], wo1[:, bass.ds(g, 1), :].rearrange("p o e -> p (o e)")).then_inc(s_sto_dma, 16)
                if nxt:
                    sp.wait_ge(s_sts_dma, upto(80 * (n + 2)))
                    c_rows1(g + b, p1, 0)

            sp.wait_ge(s_zero_ok, 4)
            groups(sp, item1)
            ov = out.rearrange("b (k p) e -> p (b k) e", p=128)
            for i in range(4):
                sp.wait_ge(s_o_ok, i + 1)
                sp.dma_start(ov[:, 4 * i:4 * i + 4, :], t3[:, 4 * i:4 * i + 4, :]).then_inc(s_out_dma, 16)
            sp.wait_ge(s_out_dma, 64)

        @block.gpsimd
        def _(pool):
            P = nc.gpsimd
            link = chained(pool, s_pool_chain)
            for idt in (ident, ident16):
                link(P.memset(idt[:, :], 0.0))
                P.affine_select(out=idt[:, :], in_=idt[:, :], compare_op=ALU.not_equal, fill=1.0, base=0,
                                pattern=[[-1, 128]], channel_multiplier=1).then_inc(s_ident_ok, 1)
            P.memset(ones[:, :], 1.0).then_inc(s_ones_ok, 1)
            pool.wait_ge(s_ones_ok, 1)
            link(P.memset(yT[:, :], 0.0))
            pool.wait_ge(s_ld_c, 16 * N_CONST)
            P.tensor_scalar(yT[:, :], yT[:, :], cols[:, BO:BO + 1], None, ALU.add).then_inc(s_yinit, 1)
            pool.wait_ge(s_lam_ok, 2)

            def item(h, b):
                own, nxt, prj = flags(h, b)
                if not own:
                    return
                n = 2 * h + b
                for qh in range(2):
                    hf = 2 * n + qh
                    for k in range(1, 8):
                        pool.wait_ge(s_exps, upto(16 * n + 8 * qh + k + 1))
                        if k == 1:
                            pool.wait_ge(s_sums, upto(hf - 1))
                        first = ering[:, 0, :, :] if k == 1 else acc[:, qh, :, :]
                        if k > 1:
                            pool.wait_ge(s_accs, upto(7 * hf + k - 1))
                        P.tensor_tensor(acc[:, qh, :, :], first, ering[:, k, :, :], ALU.add).then_inc(s_accs, 1)
                    if b == 0 and qh == 0:
                        pool.wait_ge(s_ld_wo, upto(32 * (h + 1)))
                        pool.wait_ge(s_y_mm, upto(2 * n))
                        P.tensor_tensor(wo_s[:, :], wo_raw[:, :], cols[:, LAM:LAM + 1].to_broadcast([128, E]),
                                        ALU.mult).then_inc(s_wo_ok, 1)

            heads(pool, item)

            fi = t3[:, 0:4, :].rearrange("p a c -> p (a c)").rearrange("p (k m) -> p k m", k=2)
            fc = t3[:, 4, 0:4].rearrange("p (k m) -> p k m", k=2)
            link(P.tensor_copy(fi, ib_b[:, :, :]))
            link(P.tensor_copy(fc, icol[:, :, :]))
            link(P.tensor_scalar(fb[:, :], fi[:, 0, :], float(T), None, ALU.mult))
            link(P.tensor_tensor(fb[:, :], fb[:, :], fi[:, 1, :], ALU.add))
            link(P.tensor_scalar(fcol[:, :], fc[:, 0, :], float(T), None, ALU.mult))
            link(P.tensor_tensor(fcol[:, :], fcol[:, :], fc[:, 1, :], ALU.add))
            link(P.iota(t3[:, :, :].rearrange("p a b -> p (a b)"), [[1, N]], base=0, channel_multiplier=0,
                        allow_small_or_imprecise_dtypes=True))
            link(P.iota(cols[:, PIDX:PIDX + 1], [[0, 1]], base=0, channel_multiplier=1,
                        allow_small_or_imprecise_dtypes=True))
            P.memset(cols[:, ZERO:ZERO + 1], 0.0).then_inc(s_g_ok, 1)

            def r4(i):
                return row[0:1, i:i + 4, :].rearrange("o g (j c) -> o g j c", j=4)
            link(P.memset(row[0:1, :, :], 0.0))
            for qk in range(2):
                for r in range(3):
                    link(P.tensor_copy(r4(4 * qk)[:, :, :, 8 * r:8 * r + 8],
                                       bias1[0:1, qk, :].rearrange("o (g j d) -> o g j d", g=4, j=4)))
            link(P.memset(r4(0)[:, :, :, 24:25], 1.0))
            link(P.memset(r4(4)[:, :, :, 25:27], -1.0))
            signs = row[0:1, 8:10, :].rearrange("o g (j c) -> o g j c", j=4)
            link(P.memset(signs[:, 0, :, 16:24], -1.0))
            P.memset(signs[:, 1, :, 8:16], -1.0).then_inc(s_b1_ok, 1)
            link(P.memset(wqa[:, :, :, :], 0.0))
            link(P.memset(sel[:, :], 0.0))
            for j in range(4):
                link(P.affine_select(out=sel[:, 32 * j:32 * j + 32], in_=sel[:, 32 * j:32 * j + 32],
                                     compare_op=ALU.not_equal, fill=1.0, base=-(32 * j + 8), pattern=[[0, 32]],
                                     channel_multiplier=1))
            link(P.memset(wo1[:, :, :], 0.0))
            P.memset(cols[:, ZERO:ZERO + 1], 0.0).then_inc(s_b1_ok, 1)

            def item1(g, b):
                own, nxt, prj = flags1(g, b)
                n = 2 * g + b
                if not isinstance(g, int) or n >= 1:
                    weigh1(2 * n - 1)
                if nxt:
                    pool.wait_ge(s_pv1, upto(16 * n))
                    pool.wait_ge(s_v1_ev, 1)
                    P.tensor_copy(vst[:, 1 - b, :, :, 0:8],
                                  va[:, (1 - b) * NT:(1 - b) * NT + NT, bass.ds((g + b) * 32, 32)].rearrange(
                                      "p k (j d) -> p k j d", j=4)).then_inc(s_stv_ok, 1)
                if own:
                    weigh1(2 * n)

            pool.wait_ge(s_x3_ok, TT)
            for t in (t2, t3):
                P.memset(flat(t), 0.0).then_inc(s_zero_ok, 1)
            pool.wait_ge(s_x3t_mm, 4)
            pool.wait_ge(s_msk_ok, 1)
            P.memset(flat(t1), 0.0).then_inc(s_zero_ok, 1)
            pool.wait_ge(s_p1_mm, 32)
            pool.wait_ge(s_mr_ok, 1)
            P.memset(xT[:, :], 0.0).then_inc(s_zero_ok, 1)
            def weigh1(hf):
                pool.wait_ge(s_rc1_ok, upto(4 * (hf + 1)))
                pool.wait_ge(s_os1_ok, upto(hf + 1))
                pool.wait_ge(s_y1_mm, upto(hf))
                P.tensor_tensor(on[:, :], osb[:, :], rcp[:, :], ALU.mult).then_inc(s_on1_ok, 1)

            groups(pool, item1)
            weigh1(4 * G1 - 1)

        @block.scalar
        def _(act):
            A = nc.scalar
            roots = [0]

            def root():
                roots[0] += 1
                act.wait_ge(s_var_ok, roots[0])
                A.activation(var[:, 1, :], var[:, 0, :], ACT.Sqrt).then_inc(s_root_ok, 1)

            root()
            act.wait_ge(s_wprep_mm, 1)
            A.activation(bqk[:, :, 0], PS[:, 4, 256:272], ACT.Copy)
            A.activation(bqk[:, :, 1], PS[:, 4, 288:304], ACT.Copy)
            A.activation(sw3T, PS[0:64, 4, 0:128], ACT.Copy)
            A.activation(gwT, PS[:, 4, 128:137], ACT.Copy).then_inc(s_wprep_ev, 1)
            for i in range(4):
                act.wait_ge(s_xt_mm, i + 1)
                A.activation(xT[:, 512 * i:512 * i + 512], PS[:, i, :], ACT.Copy).then_inc(s_xt_ev, 1)
            for i, (bank, dst, np) in enumerate(WPREP(wt, ew1T, ew2T, ew3T)):
                act.wait_ge(s_wprep_mm, i + 2)
                A.activation(dst, PS[0:np, bank, :], ACT.Copy).then_inc(s_wprep_ev, 1)

            def item(h, b):
                own, nxt, prj = flags(h, b)
                n = 2 * h + b
                if prj:
                    act.wait_ge(s_lo_ok, upto(4 * (n + 2)))
                for t in range(16):
                    qh, k = divmod(t, 8)
                    if own:
                        act.wait_ge(s_scores, upto(16 * n + t + 1))
                        act.wait_ge(s_pv, upto(16 * n + t - 7))
                        act.wait_ge(s_accs, upto(7 * (2 * n + qh - 1) + max(k, 1)))
                        A.activation(ering[:, k, :, :], PS[:, 2 * (t % 2):2 * (t % 2) + 2, :], ACT.Exp,
                                     scale=SCALE0).then_inc(s_exps, 1)
                    if t == 0 and prj:
                        A.activation(bcur[:, :], bqk[:, bass.ds(h + 1, 1), :].rearrange("p o i -> p (o i)"),
                                     ACT.Copy).then_inc(s_bc_ok, 1)
                    if k == 0 and (t == 8 and own or t == 0 and (not isinstance(h, int) or n >= 1)):
                        copy_out(2 * n + qh - 1)
                    if t == 1 and own:
                        ct_copy(2 * n + 1)
                    if t == 9 and nxt:
                        ct_copy(2 * (n + 1))
                    if t in (2, 4, 6, 7) and prj:
                        i = (2, 4, 6, 7).index(t)
                        act.wait_ge(s_qk_mm, upto(4 * (n + 2) + i + 1))
                        if i == 0:
                            act.wait_ge(s_maxmm, upto(16 * (n + 1)))
                            act.wait_ge(s_asm_dma, upto(192 * (n + 1)))
                            act.wait_ge(s_bc_ok, upto(n + 3))
                        bias = bcur[:, i // 2:i // 2 + 1]
                        dst = (QH, QH, KH, KH)[i]
                        A.activation(dst[:, b, (i % 2) * HF:(i % 2) * HF + HF], MISC, ACT.Identity,
                                     bias=bias).then_inc(s_hi_ok, 1)

            def copy_out(hf):
                act.wait_ge(s_pv, upto(8 * (hf + 1)))
                act.wait_ge(s_on_ok, upto(hf))
                A.activation(osb[:, :], OT, ACT.Copy).then_inc(s_os_ok, 1)

            def ct_copy(i):
                act.wait_ge(s_ct_mm, i + 1)
                act.wait_ge(s_c_dma, upto(32 * i))
                A.activation(cts[0:4, :], CT16[0:4, :], ACT.Copy).then_inc(s_ct_ev, 1)

            CT16 = MISC.bitcast(F16)[:, 0:HF]
            heads(act, item)
            copy_out(2 * last0 - 1)

            root()
            root()
            for i in range(4):
                act.wait_ge(s_x2t_mm, i + 1)
                A.activation(xT[:, 512 * i:512 * i + 512], PS[:, 4 + i, :], ACT.Copy).then_inc(s_x2t_ev, 1)
            for r in range(2):
                act.wait_ge(s_act_a, r + 1)
                A.activation(glu(t3)[0], glu(t1)[0], ACT.Exp, scale=-1.0).then_inc(s_act_b, 1)
                root()
                if r == 0:
                    for i in range(4):
                        act.wait_ge(s_zt_mm, i + 1)
                        if i == 0:
                            act.wait_ge(s_x2t_ev, 4)
                        A.activation(yT[0:64, 512 * i:512 * i + 512], PS[0:64, i, :], ACT.Identity,
                                     scale=cols[0:64, SLG:SLG + 1],
                                     bias=cols[0:64, SLB:SLB + 1]).then_inc(s_zt_ev, 1)
            act.wait_ge(s_gate_a, 1)
            A.activation(gt[:, :, 16:25], gt[:, :, 0:9], ACT.Exp, scale=-1.0).then_inc(s_gate_b, 1)
            act.wait_ge(s_gate_a, 2)
            A.activation(gt[:, :, 40:42], gt[:, :, 38:40], ACT.Exp).then_inc(s_gate_b, 1)
            root()
            for i in range(4):
                act.wait_ge(s_x3t_mm, i + 1)
                A.activation(xT[:, 512 * i:512 * i + 512], PS[:, i, :], ACT.Copy).then_inc(s_x3t_ev, 1)
            for i in range(32):
                act.wait_ge(s_p1_mm, i + 1)
                act.wait_ge(s_p1_ok, upto(i - 1))
                qk, g, blk = i // 16, (i // 4) % 4, i % 4
                A.activation(eflat[:, (i % 2) * HF:(i % 2) * HF + HF], PS[:, 4 + i % 4, :], ACT.Identity,
                             bias=pcol[:, 4 * qk + g:4 * qk + g + 1]).then_inc(s_p1_x, 1)

            def item1(g, b):
                own, nxt, prj = flags1(g, b)
                n = 2 * g + b
                for t in range(32):
                    qh = t // 16
                    if own:
                        act.wait_ge(s_scores1, upto(32 * n + t + 1))
                        act.wait_ge(s_pv1, upto(16 * n + (t - 8) // 2 + 1))
                        A.activation(ering[:, t % 8, :, :], PS[:, 2 * (t % 2):2 * (t % 2) + 2, :], ACT.Exp,
                                     scale=SCALE1).then_inc(s_exps1, 1)
                    if t == 16 and own or t == 0 and (not isinstance(g, int) or n >= 1):
                        copy_out1(2 * n + qh - 1)
                    if t == 1 and own:
                        ct_copy1(2 * n + 1)
                    if t in (2, 18) and (own if t == 18 else (not isinstance(g, int) or n >= 1)):
                        copy_totals1(2 * n + qh - 1)
                    if t == 17 and nxt:
                        ct_copy1(2 * (n + 1))

            def copy_out1(hf):
                act.wait_ge(s_pv1, upto(8 * (hf + 1)))
                act.wait_ge(s_on1_ok, upto(hf))
                A.activation(osb[:, :], OT, ACT.Copy).then_inc(s_os1_ok, 1)

            def copy_totals1(hf):
                act.wait_ge(s_sel_mm, upto(hf + 1))
                act.wait_ge(s_on1_ok, upto(hf))
                A.activation(rcp[:, :], MISC, ACT.Copy).then_inc(s_tot1_ok, 1)

            def ct_copy1(i):
                act.wait_ge(s_ct_mm1, i + 1)
                act.wait_ge(s_c_dma1, upto(64 * i))
                A.activation(cts[:, :], CT16[0:8, :], ACT.Copy).then_inc(s_ct_ev1, 1)

            groups(act, item1)
            copy_out1(4 * G1 - 1)
            copy_totals1(4 * G1 - 1)
            root()
            for i in range(4):
                act.wait_ge(s_x4t_mm, i + 1)
                A.activation(xT[:, 512 * i:512 * i + 512], PS[:, 4 + i, :], ACT.Copy).then_inc(s_x4t_ev, 1)
            for i in range(4):
                act.wait_ge(s_k_mm, i + 1)
                A.activation(yT[:, 512 * i:512 * i + 512], PS[:, i, :], ACT.Relu).then_inc(s_k_ev, 1)
            for i in range(4):
                act.wait_ge(s_r_mm, i + 1)
                A.activation(t1[:, 4 * i:4 * i + 4, :].rearrange("p a b -> p (a b)"), PS[:, 4 + i, :], ACT.Exp,
                             scale=-1.0).then_inc(s_r_ev, 1)

        @block.vector
        def _(dve):
            V = nc.vector
            link = chained(dve, s_dve_chain)
            A3 = lambda ap, n: ap.unsqueeze(1).to_broadcast([128, n, ap.shape[1]])
            B3 = lambda ap, w: ap.unsqueeze(2).to_broadcast([128, ap.shape[1], w])

            def stats(tile):
                for i in range(TT):
                    ins = V.bn_stats(st6[:, i, :], tile(i))
                link(ins)
                for i in range(TT):
                    ins = V.bn_aggr(mv[:, i, :], st6[:, i, :])
                link(ins)
                V.tensor_scalar(var[:, 0, :], mv[:, :, 1], EPS, None, ALU.add).then_inc(s_var_ok, 1)
                norms[0] += 1
                dve.wait_ge(s_root_ok, norms[0])
                link(V.reciprocal(rstd[:, :], var[:, 1, :]))
                link(V.tensor_tensor(var[:, 1, :], rstd[:, :], rstd[:, :], ALU.mult))
                link(V.tensor_tensor(var[:, 1, :], var[:, 1, :], var[:, 0, :], ALU.mult))
                link(V.tensor_scalar(var[:, 1, :], var[:, 1, :], -0.5, 1.5, ALU.mult, ALU.add))
                link(V.tensor_tensor(rstd[:, :], rstd[:, :], var[:, 1, :], ALU.mult))

            norms = [0]
            for b in range(2):
                for part in range(2):
                    V.memset(KB[64:66, b, part, :], -1.0).then_inc(s_kb_ok, 1)

            dve.wait_ge(s_ld_x, 64)
            stats(lambda i: x[:, i, :])
            for i in range(TT):
                V.tensor_scalar(t1[:, i, :], x[:, i, :], mv[:, i, 0:1], rstd[:, i:i + 1], ALU.subtract,
                                ALU.mult).then_inc(s_xn_ok, 1)
            V.memset(cols[0:64, LAM:LAM + 1], 1.0).then_inc(s_lam_ok, 1)
            dve.wait_ge(s_ld_c, 16 * N_CONST)
            V.tensor_scalar(cols[64:128, LAM:LAM + 1], cols[64:128, LAM:LAM + 1], -1.0, None,
                            ALU.mult).then_inc(s_lam_ok, 1)

            def item(h, b):
                own, nxt, prj = flags(h, b)
                n = 2 * h + b
                m = n + 1
                for t in range(16):
                    qh, k = divmod(t, 8)
                    qt, kh = k // 2, k % 2
                    if nxt:
                        dve.wait_ge(s_maxmm, upto(16 * m + t + 1))
                        part = mxp[:, qh, 0:16].rearrange("p (s q h) -> p s q h", s=2, h=2)
                        V.reduce_max(part[:, :, qt, kh:kh + 1].rearrange("p s o -> p (s o)"), MX,
                                     AX.X).then_inc(s_maxed, 1)
                    if t in (2, 4, 6, 7) and prj:
                        i = (2, 4, 6, 7).index(t)
                        dve.wait_ge(s_hi_ok, upto(4 * (n + 2) + i + 1))
                        hi, lo = ((QH, QL), (QH, QL), (KH, KL), (KH, KL))[i]
                        at = slice((i % 2) * HF, (i % 2) * HF + HF)
                        V.scalar_tensor_tensor(out=lo[:, b, at], in0=MISC, scalar=bcur[:, i // 2:i // 2 + 1],
                                               in1=hi[:, b, at], op0=ALU.add, op1=ALU.subtract).then_inc(s_lo_ok, 1)
                    if t in (3, 11) and (own if t == 11 else (not isinstance(h, int) or n >= 1)):
                        normalise(2 * n + qh - 1)
                    if t in (5, 13) and (own if t == 13 else (not isinstance(h, int) or n >= 1)):
                        add_out(2 * n + qh - 1, (b if t == 13 else 1 - b), 1 - qh)
                    if t == 10 and nxt:
                        dve.wait_ge(s_v_mm, upto(m + 1))
                        dve.wait_ge(s_pv, upto(16 * n))
                        hv = h + b
                        V.tensor_tensor(vslot[:, 1 - b, :, :], MISC.rearrange("p (k d) -> p k d", d=D0),
                                        bv_b[:, bass.ds(hv * D0, D0)].unsqueeze(1).to_broadcast([128, NT, D0]),
                                        ALU.add).then_inc(s_v_ev, 1)
                    if k == 7 and nxt:
                        row_max(m, qh)

            def row_max(m, qh):
                hf = 2 * m + qh
                dve.wait_ge(s_maxed, upto(16 * m + 8 * (qh + 1)))
                V.reduce_max(cm[:, 0:8], mxp[:, qh, 0:16].rearrange("p (a h) -> p a h", h=2),
                             AX.X).then_inc(s_cmax, 1)
                dve.wait_ge(s_cmax, upto(hf + 1))
                dve.wait_ge(s_ct_mm, upto(hf))
                c4 = c16[:, 0:16].rearrange("p (q s l) -> p s l q", s=2, l=2)
                cmv = cm[:, 0:8].rearrange("p (s q) -> p s q", s=2)
                V.tensor_copy(c4[:, :, 0, :], cmv).then_inc(s_chi, 1)
                dve.wait_ge(s_chi, upto(hf + 1))
                V.tensor_tensor(c4[:, :, 1, :], cmv, c4[:, :, 0, :], ALU.subtract).then_inc(s_c_ok, 1)

            def normalise(hf):
                dve.wait_ge(s_sums, upto(hf + 1))
                V.reciprocal(rcp[:, :], MISC).then_inc(s_rc_ok, 1)
                dve.wait_ge(s_rc_ok, upto(hf + 1))
                dve.wait_ge(s_os_ok, upto(hf + 1))
                dve.wait_ge(s_y_mm, upto(hf))
                V.tensor_tensor(on[:, :], osb[:, :], rcp[:, :], ALU.mult).then_inc(s_on_ok, 1)

            def add_out(hf, b, qh):
                at = slice(b * T + qh * HF, b * T + qh * HF + HF)
                dve.wait_ge(s_y_mm, upto(hf + 1))
                if isinstance(hf, int) and hf == 0:
                    dve.wait_ge(s_yinit, 1)
                dve.wait_ge(s_y_ok, upto(hf - 3))
                V.tensor_tensor(yT[:, at], yT[:, at], MISC, ALU.add).then_inc(s_y_ok, 1)

            heads(dve, item)
            normalise(2 * last0 - 1)
            add_out(2 * last0 - 1, 1, 1)

            link(V.tensor_scalar(gam_b[:, :], gam_b[:, :], OUT_SCALE, None, ALU.mult))
            link(V.tensor_scalar(bet_b[:, :], bet_b[:, :], OUT_SCALE, None, ALU.mult))
            link(V.tensor_tensor(x[:, :, :], x[:, :, :], A3(bet_b[:, :], TT), ALU.add))

            def psum_tile(base):
                return lambda i: PS[:, base + i // 4, (i % 4) * 128:(i % 4) * 128 + 128]
            dve.wait_ge(s_yt_mm, 4)
            pt = psum_tile(0)
            stats(pt)
            for i in range(TT):
                ins = V.tensor_scalar(t1[:, i, :], pt(i), mv[:, i, 0:1], rstd[:, i:i + 1], ALU.subtract, ALU.mult)
            link(ins)
            link(V.tensor_tensor(t1[:, :, :], t1[:, :, :], A3(gam_b[:, :], TT), ALU.mult))
            link(V.tensor_tensor(x[:, :, :], x[:, :, :], t1[:, :, :], ALU.add))
            stats(lambda i: x[:, i, :])
            for i in range(TT):
                V.tensor_scalar(t2[:, i, :], x[:, i, :], mv[:, i, 0:1], rstd[:, i:i + 1], ALU.subtract,
                                ALU.mult).then_inc(s_x2_ok, 1)
            dve.wait_ge(s_g_ok, 1)
            Gm = eflat[:, 0:4096].rearrange("p (i m) -> p i m", m=M)
            G2 = eflat[:, 4096:8192].rearrange("p (k n) -> p k n", n=N)
            for i in range(TT):
                V.tensor_scalar(Gm[:, i, :], fb[:, :], float(128 * i), cols[:, PIDX:PIDX + 1], ALU.subtract,
                                ALU.is_equal)
            for k in range(2):
                ins = V.tensor_scalar(G2[:, k, :], t3[:, :, :].rearrange("p a b -> p (a b)"), fcol[:, k:k + 1], None,
                                      ALU.is_equal)
            ins.then_inc(s_g_ok, 1)
            dve.wait_ge(s_g_ok, 2)

            H, Hh = glu(t1)
            e1, g1 = glu(t3)

            def glu_norm(r):
                dve.wait_ge(s_act_b, r + 1)
                link(V.tensor_scalar(e1, e1, 1.0, None, ALU.add))
                link(V.reciprocal(e1, e1))
                link(V.tensor_tensor(e1, e1, H, ALU.mult))
                link(V.tensor_tensor(e1, e1, Hh, ALU.mult))
                stats(lambda i: e1[:, i, :])
                link(V.tensor_tensor(e1, e1, B3(mv[:, :, 0], HE), ALU.subtract))
                return V.tensor_tensor(e1, e1, B3(rstd[:, :], HE), ALU.mult)

            dve.wait_ge(s_h_mm, 4)
            hp = PS[:, 0:4, :].rearrange("p a (i c) -> p (a i) c", c=128)
            V.tensor_tensor(H, hp[:, :, 0:64], A3(sb12_b[:, 0:64], TT), ALU.add).then_inc(s_act_a, 1)
            V.tensor_tensor(Hh, hp[:, :, 64:128], A3(sb12_b[:, 64:128], TT), ALU.add).then_inc(s_h_ev, 1)
            dve.wait_ge(s_h_ev, 1)
            glu_norm(0).then_inc(s_z_ok, 1)
            dve.wait_ge(s_gat_mm, 1)
            xm = va[:, 0:2, :].rearrange("p a b -> p (a b)")
            V.tensor_copy(xm, PS[:, 4, 0:M]).then_inc(s_gat_ev, 1)
            dve.wait_ge(s_sh_mm, 4)
            V.tensor_tensor(t2[:, :, :], PS[:, 0:4, :].rearrange("p a (i c) -> p (a i) c", c=128),
                            A3(sb3_b[:, :], TT), ALU.add).then_inc(s_sh_ev, 1)
            dve.wait_ge(s_m_mm, 2)
            eh = lambda v: v.rearrange("p (k e) c -> p k (e c)", k=2)
            dve.wait_ge(s_zt_mm, 4)
            for k in range(2):
                ins = V.tensor_tensor(H[:, 8 * k:8 * k + 8, :], PS[:, 4 + k, :].rearrange("p (e c) -> p e c", c=HE),
                                      eb1_b[:, :].rearrange("p (e c) -> p e c", c=HE), ALU.add)
            ins.then_inc(s_act_a, 1)
            for k in range(2):
                ins = V.tensor_tensor(Hh[:, 8 * k:8 * k + 8, :], PS[:, 6 + k, :].rearrange("p (e c) -> p e c", c=HE),
                                      eb2_b[:, :].rearrange("p (e c) -> p e c", c=HE), ALU.add)
            link(ins)
            link(glu_norm(1))
            link(V.tensor_tensor(e1, e1, A3(selg_b[:, :], TT), ALU.mult))
            link(V.tensor_tensor(e1, e1, A3(selb_b[:, :], TT), ALU.add))
            dve.wait_ge(s_m_mm, 3)
            V.tensor_tensor(gt[:, :, 0:9], PS[:, 0, 0:18].rearrange("p (k c) -> p k c", c=9),
                            A3(gb_b[:, :], 2), ALU.add).then_inc(s_gate_a, 1)
            dve.wait_ge(s_gate_b, 1)
            link(V.tensor_scalar(gt[:, :, 16:25], gt[:, :, 16:25], 1.0, None, ALU.add))
            link(V.reciprocal(gt[:, :, 0:9], gt[:, :, 16:25]))
            link(V.tensor_tensor(gt[:, :, 9:17], gt[:, :, 1:9], A3(xb_b[:, :], 2), ALU.add))
            link(V.reduce_max(gt[:, :, 17:18], gt[:, :, 9:17], AX.X))
            link(V.tensor_tensor(gt[:, :, 18:26], gt[:, :, 9:17], gt[:, :, 17:18].to_broadcast([128, 2, 8]),
                                 ALU.is_equal))
            for e in range(NX):
                ins = V.tensor_scalar(gt[:, :, 18 + e:19 + e], gt[:, :, 18 + e:19 + e], float(NX - e), None, ALU.mult)
            link(ins)
            link(V.reduce_max(gt[:, :, 17:18], gt[:, :, 18:26], AX.X))
            link(V.tensor_tensor(gt[:, :, 26:34], gt[:, :, 18:26], gt[:, :, 17:18].to_broadcast([128, 2, 8]),
                                 ALU.is_equal))
            link(V.tensor_tensor(gt[:, :, 18:26], gt[:, :, 26:34], gt[:, :, 1:9], ALU.mult))
            link(V.reduce_sum(gt[:, :, 34:35], gt[:, :, 18:26], AX.X))
            link(V.tensor_tensor(gt[:, :, 35:36], gt[:, :, 34:35], gt[:, :, 0:1], ALU.max))
            V.tensor_tensor(gt[:, :, 38:39], gt[:, :, 0:1], gt[:, :, 35:36], ALU.subtract)
            V.tensor_tensor(gt[:, :, 39:40], gt[:, :, 34:35], gt[:, :, 35:36],
                            ALU.subtract).then_inc(s_gate_a, 1)
            for k in range(2):
                ins = V.tensor_tensor(e1[:, 8 * k:8 * k + 8, :], e1[:, 8 * k:8 * k + 8, :],
                                      gt[:, k, 26:34].unsqueeze(2).to_broadcast([128, 8, HE]), ALU.mult)
            ins.then_inc(s_zs_ok, 1)
            dve.wait_ge(s_gate_b, 2)
            link(V.reduce_sum(gt[:, :, 42:43], gt[:, :, 40:42], AX.X))
            link(V.reciprocal(gt[:, :, 43:44], gt[:, :, 42:43]))
            link(V.tensor_tensor(gt[:, :, 44:46], gt[:, :, 40:42], gt[:, :, 43:44].to_broadcast([128, 2, 2]),
                                 ALU.mult))
            zT = yT[0:64, :].rearrange("p (e m) -> p e m", e=NX)
            for i in range(4):
                dve.wait_ge(s_zst_mm, i + 1)
                if i == 0:
                    dve.wait_ge(s_sh_mm, 4)
                V.tensor_copy(zT[:, 2 * i:2 * i + 2, :].rearrange("p e m -> p (e m)"),
                              PS[0:64, i, :]).then_inc(s_zst_ev, 1)
            dve.wait_ge(s_zst_mm, 5)
            ohT = va[0:8, 2:4, :].rearrange("p a b -> p (a b)")
            V.tensor_copy(ohT, PS[0:8, 4, 0:M]).then_inc(s_zst_ev, 1)
            F = va[:, 4:8, :].rearrange("p a b -> p (a b)").rearrange("p (k c) -> p k c", k=2)
            dve.wait_ge(s_eo_mm, 1)
            for k in range(2):
                V.tensor_scalar(F[:, k, 0:128], PS[:, 5, k * 128:k * 128 + 128], gt[:, k, 45:46], None, ALU.mult)
            V.tensor_copy(F[:, :, 128:129], gt[:, :, 44:45])
            V.memset(F[:, :, 129:130], 1.0).then_inc(s_eo_ok, 1)
            for i in range(6):
                nt = min(3, TT - 3 * i)
                dve.wait_ge(s_sc_mm, i + 1)
                ps = PS[:, i, 0:nt * 130].rearrange("p (q c) -> p q c", c=130)
                cn = st6[:, 3 * i:3 * i + nt, :]
                link(V.tensor_scalar(cn[:, :, 0:1], ps[:, :, 129:130], 1.0, None, ALU.max))
                link(V.reciprocal(cn[:, :, 1:2], cn[:, :, 0:1]))
                link(V.tensor_scalar(cn[:, :, 2:3], ps[:, :, 129:130], 0.0, None, ALU.is_equal))
                link(V.tensor_tensor(cn[:, :, 3:4], ps[:, :, 128:129], cn[:, :, 1:2], ALU.mult))
                link(V.tensor_tensor(cn[:, :, 2:3], cn[:, :, 2:3], cn[:, :, 3:4], ALU.add))
                for q in range(nt):
                    ti = 3 * i + q
                    V.tensor_scalar(t2[:, ti, :], t2[:, ti, :], cn[:, q, 2:3], None, ALU.mult)
                    ins = V.scalar_tensor_tensor(out=x[:, ti, :], in0=ps[:, q, 0:128], scalar=cn[:, q, 1:2],
                                                 in1=x[:, ti, :], op0=ALU.mult, op1=ALU.add)
                link(ins)
            link(V.tensor_tensor(x[:, :, :], x[:, :, :], t2[:, :, :], ALU.add))
            stats(lambda i: x[:, i, :])
            for i in range(TT):
                V.tensor_scalar(t1[:, i, :], x[:, i, :], mv[:, i, 0:1], rstd[:, i:i + 1], ALU.subtract,
                                ALU.mult).then_inc(s_x3_ok, 1)

            dve.wait_ge(s_b1_mm, 1)
            V.tensor_copy(pcol[:, :], PS[:, 7, 0:10]).then_inc(s_b1_ev, 1)
            dve.wait_ge(s_b1_ok, 2)
            for qk in range(2):
                for r in range(3):
                    ins = V.tensor_copy(
                        wqa[:, qk, :, :].rearrange("p g (j c) -> p (g j) c", j=4)[:, :, 8 * r:8 * r + 8],
                        wt[:, WQT + qk, :].rearrange("p (h d) -> p h d", d=8))
            ins.then_inc(s_wqa_ok, 1)
            dve.wait_ge(s_x3_ok, TT)
            link(V.tensor_scalar(kmask[:, :], t1[:, :, 0], 0.0, None, ALU.not_equal))
            dve.wait_ge(s_x3t_ev, 4)
            V.tensor_scalar(mrow[0:1, :], xT[0:1, :], 0.0, MASKED, ALU.is_equal, ALU.mult).then_inc(s_mr_ok, 1)
            for b in range(2):
                V.tensor_copy(vst[:, b, :, :, 8:32],
                              kmask[:, b * NT:b * NT + NT].unsqueeze(2).unsqueeze(3).to_broadcast([128, NT, 4, 24])
                              ).then_inc(s_msk_ok, 1)
            dve.wait_ge(s_v1_mm, 4)
            dve.wait_ge(s_x3t_mm, 4)
            link(V.tensor_tensor(va[:, :, :], PS[:, 4:8, :].rearrange("p a (i c) -> p (a i) c", c=128),
                                 A3(wvb_b[:, :], TT), ALU.add))
            V.tensor_tensor(va[:, :, :], va[:, :, :], B3(kmask[:, :], E), ALU.mult).then_inc(s_v1_ev, 1)
            tmp16 = eflat[:, 2 * HF:3 * HF].bitcast(F16)
            for i in range(32):
                qk, g, blk = i // 16, (i // 4) % 4, i % 4
                xs = eflat[:, (i % 2) * HF:(i % 2) * HF + HF]
                hs = tmp16[:, (i % 2) * HF:(i % 2) * HF + HF]
                dve.wait_ge(s_p1_x, i + 1)
                link(V.tensor_copy(hs, xs))
                V.scalar_tensor_tensor(out=(QN, KN)[qk][:, g, blk * HF:blk * HF + HF], in0=hs,
                                       scalar=pcol[:, 8 + qk:9 + qk], in1=xs, op0=ALU.mult,
                                       op1=ALU.add).then_inc(s_p1_ok, 1)

            def item1(g, b):
                own, nxt, prj = flags1(g, b)
                n = 2 * g + b
                m = n + 1
                for t in range(32):
                    qh, u = divmod(t, 16)
                    qt, kh, hp = u // 4, (u // 2) % 2, u % 2
                    if nxt:
                        part = mxp[:, qh, :].rearrange("p (s q h) -> p s q h", s=4, h=2)
                        for i in range(2):
                            dve.wait_ge(s_max1, upto(64 * m + 2 * t + i + 1))
                            V.reduce_max(part[:, 2 * hp + i, qt, kh:kh + 1], MX[:, i, :], AX.X).then_inc(s_maxed1, 1)
                    if u in (3, 4, 5, 6) and (own if qh else (not isinstance(g, int) or n >= 1)):
                        normalise1(2 * n + qh - 1, u - 3)
                    if u == 9 and (own if qh else (not isinstance(g, int) or n >= 1)):
                        add_out1(2 * n + qh - 1, (b if qh else 1 - b), 1 - qh)
                    if u == 15 and nxt:
                        row_max1(m, qh)

            def row_max1(m, qh):
                hf = 2 * m + qh
                dve.wait_ge(s_maxed1, upto(64 * m + 32 * (qh + 1)))
                V.reduce_max(cm[:, :], mxp[:, qh, :].rearrange("p (a h) -> p a h", h=2),
                             AX.X).then_inc(s_cmax1, 1)
                dve.wait_ge(s_cmax1, upto(hf + 1))
                dve.wait_ge(s_ct_mm1, upto(hf))
                c4 = c16[:, :].rearrange("p (q s l) -> p s l q", s=4, l=2)
                cmv = cm[:, :].rearrange("p (s q) -> p s q", s=4)
                V.tensor_copy(c4[:, :, 0, :], cmv).then_inc(s_chi1, 1)
                dve.wait_ge(s_chi1, upto(hf + 1))
                V.tensor_tensor(c4[:, :, 1, :], cmv, c4[:, :, 0, :], ALU.subtract).then_inc(s_c_ok1, 1)

            def normalise1(hf, c):
                at = slice(c * HF // 4, (c + 1) * HF // 4)
                dve.wait_ge(s_tot1_ok, upto(hf + 1))
                V.reciprocal(rcp[:, at], rcp[:, at]).then_inc(s_rc1_ok, 1)

            def add_out1(hf, b, qh):
                at = slice(b * T + qh * HF, b * T + qh * HF + HF)
                dve.wait_ge(s_y1_mm, upto(hf + 1))
                dve.wait_ge(s_y1_ok, upto(hf - 3))
                V.tensor_tensor(yT[:, at], yT[:, at], MISC, ALU.add).then_inc(s_y1_ok, 1)

            dve.wait_ge(s_eo_mm, 1)
            link(V.memset(yT[:, :], 0.0))
            link(V.tensor_scalar(yT[:, :], yT[:, :], cols[:, WOB:WOB + 1], None, ALU.add))
            groups(dve, item1)
            for c in range(4):
                normalise1(4 * G1 - 1, c)
            add_out1(4 * G1 - 1, 1, 1)

            dve.wait_ge(s_z1t_mm, 4)
            link(V.tensor_tensor(x[:, :, :], x[:, :, :], PS[:, 0:4, :].rearrange("p a (i c) -> p (a i) c", c=128),
                                 ALU.add))
            stats(lambda i: x[:, i, :])
            for i in range(TT):
                V.tensor_scalar(t1[:, i, :], x[:, i, :], mv[:, i, 0:1], rstd[:, i:i + 1], ALU.subtract,
                                ALU.mult).then_inc(s_x4_ok, 1)
            link(V.tensor_scalar(cols[:, OMR:OMR + 1], cols[:, MUR:MUR + 1], -1.0, 1.0, ALU.mult, ALU.add))
            link(V.tensor_scalar(cols[:, OMK:OMK + 1], cols[:, MUK:MUK + 1], -1.0, 1.0, ALU.mult, ALU.add))
            dve.wait_ge(s_x4t_ev, 4)
            t2f, t3f, vaf = flat(t2), flat(t3), flat(va)
            for mu, om, dst in ((MUK, OMK, t3f), (MUR, OMR, vaf)):
                link(V.tensor_scalar(dst, xT[:, :], cols[:, mu:mu + 1], None, ALU.mult))
                for b in range(2):
                    ins = V.scalar_tensor_tensor(
                        out=dst[:, b * T + 1:b * T + T], in0=xT[:, b * T:b * T + T - 1], scalar=cols[:, om:om + 1],
                        in1=dst[:, b * T + 1:b * T + T], op0=ALU.mult, op1=ALU.add)
                ins.then_inc(s_xr_ok, 1)
            for i in range(4):
                dve.wait_ge(s_k_ev, i + 1)
                at = slice(512 * i, 512 * i + 512)
                V.tensor_tensor(yT[:, at], yT[:, at], yT[:, at], ALU.mult).then_inc(s_k2_ok, 1)
            for i in range(4):
                dve.wait_ge(s_r_ev, i + 1)
                q = t1[:, 4 * i:4 * i + 4, :].rearrange("p a b -> p (a b)")
                link(V.tensor_scalar(q, q, 1.0, None, ALU.add))
                link(V.reciprocal(q, q))
                dve.wait_ge(s_o_mm, i + 1)
                link(V.tensor_tensor(t2f[:, 512 * i:512 * i + 512], PS[:, i, :], q, ALU.mult))
                V.tensor_tensor(t3f[:, 512 * i:512 * i + 512], t2f[:, 512 * i:512 * i + 512],
                                x[:, 4 * i:4 * i + 4, :].rearrange("p a b -> p (a b)"),
                                ALU.add).then_inc(s_o_ok, 1)

        @block.tensor
        def _(pe):
            MM = nc.tensor.matmul
            TR = nc.tensor.transpose

            pe.wait_ge(s_ident_ok, 2)
            pe.wait_ge(s_ld_w, 16 * N_W)
            TR(PS[:, 4, 256:272], eflat[0:16, 2900:3028], ident[0:16, 0:16])
            TR(PS[:, 4, 288:304], eflat[0:16, 3028:3156], ident[0:16, 0:16])
            TR(PS[0:64, 4, 0:128], eflat[:, 2816:2880], ident[:, :])
            TR(PS[:, 4, 128:137], eflat[0:9, 1024:1152], ident[0:9, 0:9]).then_inc(s_wprep_mm, 1)
            for i in range(TT):
                pe.wait_ge(s_xn_ok, i + 1)
                mm = TR(PS[:, i // 4, (i % 4) * 128:(i % 4) * 128 + 128], t1[:, i, :], ident[:, :])
                if i % 4 == 3:
                    mm.then_inc(s_xt_mm, 1)
            raw = [[0, 1, 2, 3], [4, 5, 6, 7], [9, 10, 11, 12], [13, 14, 15, 16]]
            for i in range(6):
                bank = (5, 6, 7, 0, 1, 2)[i]
                if bank < 3:
                    pe.wait_ge(s_xt_ev, bank + 1)
                for j in range(4):
                    if i < 4:
                        src = eflat[:, 128 * raw[i][j]:128 * raw[i][j] + 128]
                        mm = TR(PS[:, bank, 128 * j:128 * j + 128], src, ident[:, :])
                    else:
                        e = (i - 4) * 4 + j
                        mm = TR(PS[0:64, bank, 128 * j:128 * j + 128], eflat[:, 2304 + 64 * e:2304 + 64 * e + 64],
                                ident[:, :])
                mm.then_inc(s_wprep_mm, 1)
            pe.wait_ge(s_wprep_ev, 7)
            pe.wait_ge(s_xt_ev, 4)
            pe.wait_ge(s_kb_ok, 4)
            pe.wait_ge(s_ones_ok, 1)

            def item(h, b):
                own, nxt, prj = flags(h, b)
                n = 2 * h + b
                m = n + 1
                later = not isinstance(h, int) or n >= 1
                for t in range(16):
                    qh, k = divmod(t, 8)
                    if own:
                        if t == 0:
                            pe.wait_ge(s_asm_dma, upto(192 * (n + 1)))
                            pe.wait_ge(s_c_dma, upto(32 * (2 * n + 1)))
                        if t == 8:
                            pe.wait_ge(s_c_dma, upto(32 * (2 * n + 2)))
                        pe.wait_ge(s_exps, upto(16 * n + t - 1))
                        for part in range(2):
                            dst = PS[:, 2 * (t % 2) + part, :]
                            MM(dst, KA[:, b, part, k * 128:k * 128 + 128], QA[:, b, part, qh * HF:qh * HF + HF],
                               start=True, stop=False)
                            mm = MM(dst, KB[0:66, b, part, k * 128:k * 128 + 128],
                                    QB[0:66, b, part, qh * HF:qh * HF + HF], start=False, stop=True)
                        mm.then_inc(s_scores, 1)
                    if nxt:
                        qt, kh = t // 2, t % 2
                        if t == 0:
                            pe.wait_ge(s_lo_ok, upto(4 * (m + 1)))
                        pe.wait_ge(s_maxed, upto(16 * m + t))
                        for part in range(2):
                            r = slice(64 * part, 64 * part + 64)
                            mm = MM(PS[:, 4 + part, :], QH[r, 1 - b, qt * 128:qt * 128 + 128],
                                    KH[r, 1 - b, kh * HF:kh * HF + HF], start=True, stop=True)
                        mm.then_inc(s_maxmm, 1)
                    if t == 0 and later:
                        values(n - 1, 1 - b, 15)
                    if t > 0 and own:
                        values(n, b, t - 1)
                    if t == 1 and own:
                        pe.wait_ge(s_y_ok, upto(2 * n - 1))
                        spread(2 * n + 1)
                    if t == 2 and prj:
                        pe.wait_ge(s_ct_ev, upto(2 * n + 2))
                        pe.wait_ge(s_v_ev, upto(n + 1))
                        pe.wait_ge(s_ld_wqk, upto(32 * (h + 2)))
                        project(n, b, 0)
                    if t == 3 and later:
                        pe.wait_ge(s_lo_ok, upto(4 * (n + 2) + 1 if prj else 0))
                        pe.wait_ge(s_ct_ev, upto(2 * n + 2 if own else 0))
                        total(2 * n - 1, 1)
                    if t == 4 and prj:
                        pe.wait_ge(s_lo_ok, upto(4 * (n + 2) + 1))
                        pe.wait_ge(s_rc_ok, upto(2 * n))
                        project(n, b, 1)
                    if t == 5 and later:
                        pe.wait_ge(s_lo_ok, upto(4 * (n + 2) + 2 if prj else 0))
                        to_out(2 * n - 1, None)
                    if t == 6 and prj:
                        pe.wait_ge(s_lo_ok, upto(4 * (n + 2) + 2))
                        pe.wait_ge(s_y_ok, upto(2 * n))
                        project(n, b, 2)
                    if t == 7 and prj:
                        pe.wait_ge(s_lo_ok, upto(4 * (n + 2) + 3))
                        project(n, b, 3)
                    if t == 9 and nxt:
                        pe.wait_ge(s_lo_ok, upto(4 * (n + 3) if prj else 0))
                        pe.wait_ge(s_y_ok, upto(2 * n))
                        spread(2 * m)
                    if t == 10 and nxt:
                        pe.wait_ge(s_ct_ev, upto(2 * m + 1))
                        pe.wait_ge(s_ld_wv, upto(16 * (h + b + 1)))
                        for i in range(NT):
                            mm = MM(MISC[:, i * D0:i * D0 + D0],
                                    xT[:, (1 - b) * T + i * 128:(1 - b) * T + i * 128 + 128], wv_s[:, :],
                                    start=True, stop=True)
                        mm.then_inc(s_v_mm, 1)
                    if t == 11 and own:
                        if nxt:
                            pe.wait_ge(s_v_ev, upto(m + 1))
                        else:
                            pe.wait_ge(s_y_ok, upto(2 * n))
                        total(2 * n, 0)
                    if t == 13 and own:
                        pe.wait_ge(s_rc_ok, upto(2 * n + 1))
                        to_out(2 * n, h)

            def values(n, b, t):
                qh, k = divmod(t, 8)
                if t == 0:
                    pe.wait_ge(s_v_ev, upto(n + 1))
                if k == 0:
                    pe.wait_ge(s_os_ok, upto(2 * n + qh))
                pe.wait_ge(s_exps, upto(16 * n + t + 1))
                for part in range(2):
                    mm = MM(OT[64 * part:64 * part + 64, :], vslot[:, b, k, :], ering[:, k, part, :],
                            start=(k == 0), stop=(k == 7))
                mm.then_inc(s_pv, 1)

            def spread(hf):
                pe.wait_ge(s_c_ok, upto(hf + 1))
                for q in range(4):
                    mm = TR(MISC.bitcast(F16)[0:4, q * 128:q * 128 + 128], c16[:, 4 * q:4 * q + 4], ident16[:, :])
                mm.then_inc(s_ct_mm, 1)

            def project(n, b, i):
                w = (wq_s, wq_s, wk_s, wk_s)[i]
                at = b * T + (i % 2) * HF
                MM(MISC, w[:, :], xT[:, at:at + HF], start=True, stop=True).then_inc(s_qk_mm, 1)

            def total(hf, qh):
                pe.wait_ge(s_accs, upto(7 * (hf + 1)))
                for part in range(2):
                    mm = MM(MISC[64 * part:64 * part + 64, :], ones[:, :], acc[:, qh, part, :], start=True, stop=True)
                mm.then_inc(s_sums, 1)

            def to_out(hf, h):
                pe.wait_ge(s_on_ok, upto(hf + 1))
                pe.wait_ge(s_rc_ok, upto(hf + 1))
                if h is not None:
                    pe.wait_ge(s_wo_ok, upto(h + 1))
                MM(MISC, wo_s[:, :], on[:, :], start=True, stop=True).then_inc(s_y_mm, 1)

            heads(pe, item)
            values(last0 - 1, 1, 15)
            pe.wait_ge(s_y_ok, 2 * last0 - 1)
            total(2 * last0 - 1, 1)
            to_out(2 * last0 - 1, None)

            def spot(i, base=0, rows=128, w=128):
                return PS[0:rows, base + i // 4, (i % 4) * 128:(i % 4) * 128 + w]

            def tiles(done, op):
                for i in range(TT):
                    mm = op(i)
                    if i % 4 == 3:
                        mm.then_inc(done, 1)

            def tok(v, i):
                return v[:, i * 128:i * 128 + 128]

            pe.wait_ge(s_y_ok, 2 * last0)
            pe.wait_ge(s_maxed, 16 * last0)
            pe.wait_ge(s_exps, 16 * last0)
            tiles(s_yt_mm, lambda i: TR(spot(i), tok(yT, i), ident[:, :]))

            def x2_tile(i):
                pe.wait_ge(s_x2_ok, i + 1)
                return TR(spot(i, 4), t2[:, i, :], ident[:, :])
            tiles(s_x2t_mm, x2_tile)
            pe.wait_ge(s_x2t_ev, 4)
            tiles(s_h_mm, lambda i: MM(spot(i), tok(xT, i), wt[:, SW12T, :], start=True, stop=True))
            pe.wait_ge(s_g_ok, 2)
            Gm = eflat[:, 0:4096].rearrange("p (i m) -> p i m", m=M)
            G2 = eflat[:, 4096:8192].rearrange("p (k n) -> p k n", n=N)
            for i in range(TT):
                mm = MM(PS[:, 4, 0:M], t2[:, i, :], Gm[:, i, :], start=(i == 0), stop=(i == TT - 1))
            mm.then_inc(s_gat_mm, 1)
            pe.wait_ge(s_z_ok, 1)
            e1 = glu(t3)[0]
            tiles(s_zt_mm, lambda i: TR(spot(i, 0, 64), e1[:, i, :], ident[:, :]))
            pe.wait_ge(s_zt_ev, 4)
            tiles(s_sh_mm, lambda i: MM(spot(i), yT[0:64, i * 128:i * 128 + 128], sw3T, start=True, stop=True))
            pe.wait_ge(s_gat_ev, 1)
            xm = va[:, 0:2, :].rearrange("p a b -> p (a b)")
            for k in range(2):
                MM(PS[:, 4 + k, :], tok(xm, k), ew1T[:, :], start=True, stop=True)
                MM(PS[:, 6 + k, :], tok(xm, k), ew2T[:, :], start=True, stop=True).then_inc(s_m_mm, 1)
            pe.wait_ge(s_sh_ev, 1)
            for k in range(2):
                mm = MM(PS[:, 0, 9 * k:9 * k + 9], tok(xm, k), gwT, start=True, stop=True)
            mm.then_inc(s_m_mm, 1)
            pe.wait_ge(s_zs_ok, 1)
            for i in range(4):
                for e in (2 * i, 2 * i + 1):
                    for k in range(2):
                        at = (e % 2) * 256 + k * 128
                        mm = TR(PS[0:64, i, at:at + 128], e1[:, 8 * k + e, :], ident[:, :])
                mm.then_inc(s_zst_mm, 1)
            for k in range(2):
                mm = TR(PS[0:8, 4, k * 128:k * 128 + 128], gt[:, k, 26:34], ident[:, :])
            mm.then_inc(s_zst_mm, 1)
            pe.wait_ge(s_zst_ev, 5)
            zT = yT[0:64, :].rearrange("p (e m) -> p e m", e=NX)
            ohT = va[0:8, 2:4, :].rearrange("p a b -> p (a b)")
            for k in range(2):
                dst = PS[:, 5, k * 128:k * 128 + 128]
                for e in range(NX):
                    MM(dst, zT[:, e, k * 128:k * 128 + 128], ew3T[:, e, :], start=(e == 0), stop=False)
                mm = MM(dst, ohT[:, k * 128:k * 128 + 128], eb3[:, :], start=False, stop=True)
            mm.then_inc(s_eo_mm, 1)
            F = va[:, 4:8, :].rearrange("p a b -> p (a b)").rearrange("p (k c) -> p k c", k=2)
            pe.wait_ge(s_eo_ok, 1)
            for i in range(TT):
                for k in range(2):
                    mm = MM(PS[:, i // 3, (i % 3) * 130:(i % 3) * 130 + 130], tok(G2[:, k, :], i), F[:, k, 0:130],
                            start=(k == 0), stop=(k == 1))
                if i % 3 == 2 or i == TT - 1:
                    mm.then_inc(s_sc_mm, 1)
            pe.wait_ge(s_b1_ok, 1)
            for i in range(10):
                mm = MM(PS[:, 7, i:i + 1], row[0:1, i, :], ones[0:1, 0:1], start=True, stop=True)
            mm.then_inc(s_b1_mm, 1)

            def x3_tile(i):
                pe.wait_ge(s_x3_ok, i + 1)
                return TR(spot(i), t1[:, i, :], ident[:, :])
            tiles(s_x3t_mm, x3_tile)
            pe.wait_ge(s_x3t_ev, 4)
            pe.wait_ge(s_b1_ev, 1)
            tiles(s_v1_mm, lambda i: MM(spot(i, 4), tok(xT, i), wt[:, WVT, :], start=True, stop=True))
            pe.wait_ge(s_v1_ev, 1)
            pe.wait_ge(s_wqa_ok, 1)
            for i in range(32):
                qk, g, blk = i // 16, (i // 4) % 4, i % 4
                pe.wait_ge(s_p1_x, upto(i - 3))
                MM(PS[:, 4 + i % 4, :], wqa[:, qk, g, :], xT[:, blk * HF:blk * HF + HF], start=True,
                   stop=True).then_inc(s_p1_mm, 1)
            pe.wait_ge(s_msk_ok, 2)
            pe.wait_ge(s_p1_x, 32)

            def item1(g, b):
                own, nxt, prj = flags1(g, b)
                n = 2 * g + b
                m = n + 1
                later = not isinstance(g, int) or n >= 1
                for t in range(32):
                    qh, u = divmod(t, 16)
                    k, hp = u // 2, u % 2
                    if own:
                        if t == 0:
                            pe.wait_ge(s_sts_dma, upto(80 * (n + 1)))
                            pe.wait_ge(s_c_dma1, upto(64 * (2 * n + 1)))
                        if t == 16:
                            pe.wait_ge(s_c_dma1, upto(64 * (2 * n + 2)))
                        pe.wait_ge(s_exps1, upto(32 * n + t - 1))
                        for i in range(2):
                            mm = MM(PS[:, 2 * (t % 2) + i, :], KS[b][:, 2 * hp + i, k * 128:k * 128 + 128],
                                    QS[:, b, qh * HF:qh * HF + HF], start=True, stop=True)
                        mm.then_inc(s_scores1, 1)
                    if nxt:
                        qt, kh = t // 4, (t // 2) % 2
                        if t == 0:
                            pe.wait_ge(s_stm_dma, upto(80 * (m + 1)))
                        for i in range(2):
                            pe.wait_ge(s_maxed1, upto(64 * m + 2 * t - 1 + i))
                            MM(PS[:, 4 + i, :], QM[1 - b][:, 2 * hp + i, qt * 128:qt * 128 + 128],
                               KM[:, 1 - b, kh * HF:kh * HF + HF], start=True, stop=True).then_inc(s_max1, 1)
                    if t == 0 and later:
                        values1(n - 1, 1 - b, 15)
                    if t > 0 and t % 2 == 0 and own:
                        values1(n, b, t // 2 - 1)
                    if t == 1 and own:
                        pe.wait_ge(s_y1_ok, upto(2 * n - 1))
                        spread1(2 * n + 1)
                    if t == 2 and later:
                        pe.wait_ge(s_ct_ev1, upto(2 * n + 2 if own else 0))
                        totals1(2 * n - 1)
                    if t == 8 and later:
                        to_out1(2 * n - 1, None)
                    if t == 17 and nxt:
                        pe.wait_ge(s_y1_ok, upto(2 * n))
                        spread1(2 * m)
                    if t == 18 and own:
                        if nxt:
                            pe.wait_ge(s_ct_ev1, upto(2 * m + 1))
                        else:
                            pe.wait_ge(s_y1_ok, upto(2 * n))
                        totals1(2 * n)
                    if t == 24 and own:
                        to_out1(2 * n, g)

            def values1(n, b, u):
                qh, k = divmod(u, 8)
                if u == 0:
                    pe.wait_ge(s_stv_ok, upto(n + 1))
                if k == 0:
                    pe.wait_ge(s_os1_ok, upto(2 * n + qh))
                pe.wait_ge(s_exps1, upto(32 * n + 2 * u + 2))
                for j in range(4):
                    mm = MM(OT[32 * j:32 * j + 32, :], vst[:, b, k, j, :], ering[:, (2 * u + j // 2) % 8, j % 2, :],
                            start=(k == 0), stop=(k == 7))
                mm.then_inc(s_pv1, 1)

            def spread1(hf):
                pe.wait_ge(s_c_ok1, upto(hf + 1))
                for q in range(4):
                    mm = TR(MISC.bitcast(F16)[0:8, q * 128:q * 128 + 128], c16[:, 8 * q:8 * q + 8], ident16[:, :])
                mm.then_inc(s_ct_mm1, 1)

            def totals1(hf):
                pe.wait_ge(s_os1_ok, upto(hf + 1))
                MM(MISC, sel[:, :], osb[:, :], start=True, stop=True).then_inc(s_sel_mm, 1)

            def to_out1(hf, g):
                pe.wait_ge(s_on1_ok, upto(hf + 1))
                pe.wait_ge(s_tot1_ok, upto(hf + 1))
                if g is not None:
                    pe.wait_ge(s_sto_dma, upto(16 * (g + 1)))
                MM(MISC, wo_s[:, :], on[:, :], start=True, stop=True).then_inc(s_y1_mm, 1)

            groups(pe, item1)
            values1(2 * G1 - 1, 1, 15)
            pe.wait_ge(s_y1_ok, upto(4 * G1 - 1))
            totals1(4 * G1 - 1)
            to_out1(4 * G1 - 1, None)

            pe.wait_ge(s_y1_ok, 4 * G1)
            pe.wait_ge(s_maxed1, 128 * G1)
            pe.wait_ge(s_exps1, 64 * G1)
            tiles(s_z1t_mm, lambda i: TR(spot(i), tok(yT, i), ident[:, :]))

            def x4_tile(i):
                pe.wait_ge(s_x4_ok, i + 1)
                return TR(spot(i, 4), t1[:, i, :], ident[:, :])
            tiles(s_x4t_mm, x4_tile)
            t3f, vaf = flat(t3), flat(va)
            pe.wait_ge(s_x4t_ev, 4)
            pe.wait_ge(s_xr_ok, 1)
            for i in range(4):
                MM(PS[:, i, :], wt[:, WCT, :], t3f[:, 512 * i:512 * i + 512], start=True,
                   stop=True).then_inc(s_k_mm, 1)
            pe.wait_ge(s_xr_ok, 2)
            tiles(s_r_mm, lambda i: MM(spot(i, 4), tok(vaf, i), wt[:, WRT, :], start=True, stop=True))

            def o_tile(i):
                pe.wait_ge(s_k2_ok, i // 4 + 1)
                return MM(spot(i), tok(yT, i), wt[:, WVV, :], start=True, stop=True)
            tiles(s_o_mm, o_tile)


N_CONST = 30
N_W = 17


def WPREP(wt, ew1T, ew2T, ew3T):
    half = [ew3T[:, 4 * i:4 * i + 4, :].rearrange("p e d -> p (e d)") for i in range(2)]
    return [(5, wt[:, 0:4, :].rearrange("p a b -> p (a b)"), 128),
            (6, wt[:, 4:8, :].rearrange("p a b -> p (a b)"), 128),
            (7, ew1T[:, :], 128), (0, ew2T[:, :], 128), (1, half[0], HE), (2, half[1], HE)]


OUT_SHAPE = (B, T, E)


def kernel(**inputs):
    import numpy as _np
    import concourse.bacc as _bacc
    from concourse import mybir as _mybir
    from concourse.bass_utils import run_bass_kernel_spmd as _run

    nc = _bacc.Bacc("TRN2", target_bir_lowering=False, num_devices=1)
    arrays, args = {}, {}
    for name in sorted(inputs):
        v = _np.ascontiguousarray(inputs[name])
        arrays[f"in_{name}"] = v
        args[name] = nc.dram_tensor(f"in_{name}", v.shape, _mybir.dt.from_np(v.dtype), kind="ExternalInput").ap()
    o = nc.dram_tensor("out_0", OUT_SHAPE, _mybir.dt.float32, kind="ExternalOutput").ap()
    two_layers(nc, args, o)
    r = _run(nc, [arrays], core_ids=[0])
    return r.results[0]["out_0"]
```
